# Optimizing a Trainium2 kernel written in Bass

```python
import numpy as np
import jax
import jax.numpy as jnp

def _softmax(x, axis=-1):
    return jax.nn.softmax(x, axis=axis)

def _gelu(x):
    return jax.nn.gelu(x, approximate=True)

def _silu(x):
    return jax.nn.silu(x)

def _sigmoid(x):
    return jax.nn.sigmoid(x)

def _layernorm(x, axis=-1, eps=1e-05):
    m = jnp.mean(x, axis=axis, keepdims=True)
    v = jnp.var(x, axis=axis, keepdims=True)
    return (x - m) / jnp.sqrt(v + eps)

def _scatter_add(tgt, idx, src, axis=0):
    return tgt.at[idx].add(src)

def _segment_sum(src, seg, n):
    return jax.ops.segment_sum(src, seg, n)
kernel_name = 'mk_adj_resnorm_d2_adj_r2_f117e9'

def setup_inputs(seed: int=0):
    np.random.seed(seed)
    _w = jnp.asarray

    def _rec_inputs():
        import jax
        import jax.numpy as jnp
        _gk = jax.random.key(seed)
        x = -8.776e-05 + 1 * jax.random.normal(jax.random.fold_in(_gk, 1), (10000, 128), jnp.float32)
        _w = (1.0 + jnp.arange(10000, dtype=jnp.float32)) ** (-0.5)
        _w = _w / _w.mean()
        _pij = jnp.clip(0.0016 * _w[:, None] * _w[None, :], 0.0, 1.0)
        _a = jax.random.uniform(jax.random.fold_in(_gk, 2), (10000, 10000)) < _pij
        _a = jnp.logical_or(_a, jnp.eye(10000, dtype=bool))
        _af = _a.astype(jnp.float32)
        _af = _af * jax.random.uniform(jax.random.fold_in(_gk, 3), (10000, 10000), jnp.float32, 0.05, 1)
        adj = _af
        return (x, adj)
    x, adj = _rec_inputs()

    def _L0_gnn_setup():
        import jax, jax.numpy as jnp
        import numpy as np
        N_USER = 10000
        N_ITEM = 10000
        HID = 128
        key = jax.random.key(seed)
        k1, k2, k3, k4, k5, k6, k7 = jax.random.split(key, 7)
        scale = 1.0 / np.sqrt(HID)
        return {'user_feat': jax.random.normal(k1, (N_USER, HID), dtype=jnp.float32), 'item_feat': jax.random.normal(k2, (N_ITEM, HID), dtype=jnp.float32), 'adj': jax.random.uniform(k3, (N_USER, N_ITEM), dtype=jnp.float32), 'W_item': jax.random.uniform(k4, (HID, HID), dtype=jnp.float32, minval=-scale, maxval=scale), 'b_item': jax.random.uniform(k5, (HID,), dtype=jnp.float32, minval=-scale, maxval=scale), 'W_user': jax.random.uniform(k6, (HID, HID), dtype=jnp.float32, minval=-scale, maxval=scale), 'b_user': jax.random.uniform(k7, (HID,), dtype=jnp.float32, minval=-scale, maxval=scale)}
    _L0_gnn_all = _L0_gnn_setup()
    _L0_gnn_in = {k: v for k, v in _L0_gnn_all.items() if k in ('item_feat', 'W_item', 'b_item', 'W_user', 'b_user')}
    del _L0_gnn_all

    def _L1_gnn_setup():
        import jax, jax.numpy as jnp
        import numpy as np
        N = 4096
        D = 128
        CUTOFF = 1.0
        MU = 1.0
        SIGMA = 0.5

        def sensitivity(r, mu, sigma):
            return jnp.exp(-(1.0 / r - 1.0 / mu) ** 2 / (2.0 * sigma * sigma))
        key = jax.random.key(seed)
        k_z, k_d, k_w = jax.random.split(key, 3)
        z = jax.random.normal(k_z, (N, D), dtype=jnp.float32)
        dist_matrix = jax.random.uniform(k_d, (N, N), dtype=jnp.float32) * 2.0 + 0.05
        W = jax.random.normal(k_w, (D, D), dtype=jnp.float32)
        B = jnp.zeros((D,), dtype=jnp.float32)
        return {'z': z, 'dist_matrix': dist_matrix, 'W': W, 'B': B}
    _L1_gnn_all = _L1_gnn_setup()
    _L1_gnn_in = {k: v for k, v in _L1_gnn_all.items() if k in ('W', 'B')}
    del _L1_gnn_all
    return {'x': x, 'adj': adj, 'L0_gnn_item_feat': _L0_gnn_in['item_feat'], 'L0_gnn_W_item': _L0_gnn_in['W_item'], 'L0_gnn_b_item': _L0_gnn_in['b_item'], 'L0_gnn_W_user': _L0_gnn_in['W_user'], 'L0_gnn_b_user': _L0_gnn_in['b_user'], 'L1_gnn_W': _L1_gnn_in['W'], 'L1_gnn_B': _L1_gnn_in['B']}

def reference(x, adj, L0_gnn_item_feat, L0_gnn_W_item, L0_gnn_b_item, L0_gnn_W_user, L0_gnn_b_user, L1_gnn_W, L1_gnn_B):
    import jax
    import jax.numpy as jnp

    def _L0_gnn_ref(user_feat, item_feat, adj, W_item, b_item, W_user, b_user):
        import jax, jax.numpy as jnp
        import numpy as np
        N_USER = 10000
        N_ITEM = 10000
        HID = 128
        h = item_feat @ W_item.T + b_item
        b = user_feat @ W_user.T + b_user
        return jax.nn.relu(adj @ h + b)

    def _L1_gnn_ref(z, dist_matrix, W, B):
        import jax, jax.numpy as jnp
        import numpy as np
        N = 4096
        D = 128
        CUTOFF = 1.0
        MU = 1.0
        SIGMA = 0.5

        def sensitivity(r, mu, sigma):
            return jnp.exp(-(1.0 / r - 1.0 / mu) ** 2 / (2.0 * sigma * sigma))
        msg = z @ W + B
        sens = sensitivity(dist_matrix, MU, SIGMA)
        weights = jnp.where(dist_matrix < CUTOFF, sens, 0.0)
        return weights @ msg
    x = _layernorm(x + _L0_gnn_ref(x, L0_gnn_item_feat, adj, L0_gnn_W_item, L0_gnn_b_item, L0_gnn_W_user, L0_gnn_b_user), axis=-1)
    x = _layernorm(x + _L1_gnn_ref(x, adj, L1_gnn_W, L1_gnn_B), axis=-1)
    return x

_drawn_inputs = setup_inputs


def setup_inputs(seed=0):
    import zlib

    import numpy as np

    out = dict(_drawn_inputs(seed))
    spreads = {'L1_gnn_B': (0.0, 0.379)}
    factors = {}
    for name, (base, spread) in spreads.items():
        noise = np.random.default_rng([zlib.crc32(name.encode()), seed]).standard_normal(out[name].shape)
        drawn = base * np.exp(spread * noise) if base else spread * noise
        out[name] = jnp.asarray(drawn.astype(out[name].dtype))
    for name, factor in factors.items():
        out[name] = (out[name] * factor).astype(out[name].dtype)
    return out
```

```python
import numpy as np
from contextlib import ExitStack

import concourse.bass as bass
from concourse import mybir


def two_graph_layers(nc, x, adj, item, w_item, b_item, w_user, b_user, w_msg, b_msg, out):
    F32 = mybir.dt.float32
    ALU = mybir.AluOpType
    ACT = mybir.ActivationFunctionType

    N, D = x.shape
    P = 128
    S = 32
    Q = P // S
    COLBLOCKS = 80
    QCOLS = COLBLOCKS * S
    QSTRIDE = (N - QCOLS) // (Q - 1)
    assert QSTRIDE * (Q - 1) + QCOLS == N and QSTRIDE <= QCOLS
    CHUNKS = 8
    CB = COLBLOCKS // CHUNKS
    CCOLS = CB * S
    RG = 15
    BLOCK = RG * S
    BLOCKS = 21
    BSTRIDE = (N - BLOCK) // (BLOCKS - 1)
    assert BSTRIDE * (BLOCKS - 1) + BLOCK == N and BSTRIDE <= BLOCK
    SUB = 4
    SP_ROWS = BLOCK // SUB
    CHUNK = RG * CCOLS
    NBUF = 4
    USES = CHUNKS // NBUF
    EPS = 1e-5
    TINY = 2.0 ** -60
    FIRST_DUP = QSTRIDE // S
    DUPS = COLBLOCKS - FIRST_DUP
    DVE_SQUARED = [0, 1, 2, 3, 4]
    GROUPS = COLBLOCKS // SUB

    x1_dram = nc.dram_tensor("x1_scratch", (N, D), F32, kind="Internal").ap()
    msg_dram = nc.dram_tensor("msg_scratch", (N, D), F32, kind="Internal").ap()

    def block_rows(dram, b):
        return dram[bass.ds(b * BSTRIDE, BLOCK), :].rearrange("(q p) d -> p q d", p=SP_ROWS)

    def stretch(dram, q):
        return dram[q * QSTRIDE:q * QSTRIDE + QCOLS, :].rearrange("(j p) d -> p j d", p=S)

    def adj_chunk(b, c, q):
        rows = adj[bass.ds(b * BSTRIDE, BLOCK), :].rearrange("(r p) n -> p r n", p=S)
        return rows[:, :, q * QSTRIDE + c * CCOLS:q * QSTRIDE + (c + 1) * CCOLS]

    ctx = ExitStack()
    with ctx:
        def sb(name, shape):
            return ctx.enter_context(nc.sbuf_tensor(name, shape, F32))

        def ps(name, shape):
            return ctx.enter_context(nc.psum_tensor(name, shape, F32))

        def sem(name):
            return ctx.enter_context(nc.semaphore(name))

        feat = sb("feat", [P, COLBLOCKS, D])
        raw = [sb(f"raw{i}", [P, RG, CCOLS]) for i in range(NBUF)]
        tr = [sb(f"tr{i}", [P, RG, CB, S]) for i in range(NBUF)]
        ident = sb("ident", [P, P])
        first_named = sb("first_named", [P, COLBLOCKS])
        w_item_nat = sb("w_item_nat", [D, D])
        w_user_nat = sb("w_user_nat", [D, D])
        w_item_t = sb("w_item_t", [D, D])
        w_user_t = sb("w_user_t", [D, D])
        w_msg_sb = sb("w_msg_sb", [D, D])
        b_item_bc = sb("b_item_bc", [P, D])
        b_msg_bc = sb("b_msg_bc", [P, D])
        b_user_col = sb("b_user_col", [D, 1])
        tiny = sb("tiny", [P, 1])
        minus1 = sb("minus1", [P, 1])
        minus2 = sb("minus2", [P, 1])
        x_rows = sb("x_rows", [SP_ROWS, SUB, D])
        x_t = sb("x_t", [D, SUB * P])
        z_t = sb("z_t", [D, BLOCK])
        res = sb("res", [SP_ROWS, SUB, D])
        x1_t = sb("x1_t", [D, SUB * P])
        msg = sb("msg", [SP_ROWS, SUB, D])
        stats = sb("stats", [SP_ROWS, SUB, 6])
        meanvar = sb("meanvar", [SP_ROWS, SUB, 2])
        var_eps = sb("var_eps", [SP_ROWS, SUB])
        log_var = sb("log_var", [SP_ROWS, SUB])
        rstd0 = sb("rstd0", [SP_ROWS, SUB])
        newton = sb("newton", [SP_ROWS, SUB])
        rstd = sb("rstd", [SP_ROWS, SUB])

        acc = [ps(f"acc{i}", [D, BLOCK]) for i in range(2)]
        p_xt = ps("p_xt", [D, SUB * P])
        p_z = ps("p_z", [P, SUB, D])
        p_x1t = ps("p_x1t", [D, SUB * P])
        p_msg = ps("p_msg", [P, SUB, D])

        consts_loaded = sem("consts_loaded")
        items_loaded = sem("items_loaded")
        ident_zeroed = sem("ident_zeroed")
        biases_set = sem("biases_set")
        masks_set = sem("masks_set")
        masks_ready = sem("masks_ready")
        w_transposed = sem("w_transposed")
        w_copied = sem("w_copied")
        item_transposed = sem("item_transposed")
        item_t_copied = sem("item_t_copied")
        item_product = sem("item_product")
        item_features = sem("item_features")
        features_ready = sem("features_ready")
        low_loaded = [sem(f"low_loaded{i}") for i in range(NBUF)]
        high_loaded = [sem(f"high_loaded{i}") for i in range(NBUF)]
        masked = sem("masked")
        transposed = sem("transposed")
        logged = sem("logged")
        inverted = sem("inverted")
        act_squared = sem("act_squared")
        dve_squared = sem("dve_squared")
        weighted = sem("weighted")
        multiplied = sem("multiplied")
        x_loaded = sem("x_loaded")
        x_transposed = sem("x_transposed")
        x_t_ready = sem("x_t_ready")
        sums_done = sem("sums_done")
        z_t_ready = sem("z_t_ready")
        z_transposed = sem("z_transposed")
        res_loaded = sem("res_loaded")
        res_added = sem("res_added")
        norm_step = sem("norm_step")
        var_ready = sem("var_ready")
        log_var_ready = sem("log_var_ready")
        rstd0_ready = sem("rstd0_ready")
        rstd_refined = sem("rstd_refined")
        normed = sem("normed")
        x1_transposed = sem("x1_transposed")
        x1_t_ready = sem("x1_t_ready")
        msg_product = sem("msg_product")
        msg_ready = sem("msg_ready")
        x1_stored = sem("x1_stored")
        msg_stored = sem("msg_stored")
        msg_loaded = sem("msg_loaded")
        msg_masked = sem("msg_masked")
        out_stored = sem("out_stored")

        block = ctx.enter_context(nc.Block())

        def over_blocks(eng, body):
            body(0, 0)
            with eng.Fori(1, BLOCKS - 1, 2) as b:
                body(b, 1)
                body(b + 1, 0)

        def is_start(b):
            return isinstance(b, int) and b == 0

        def load_adj(eng, layer, quadrants, loaded):
            def body(b, _):
                g = b + layer * BLOCKS
                for c in range(CHUNKS):
                    if layer or not is_start(b) or c >= NBUF:
                        eng.wait_ge(transposed, g * CHUNKS + (c + 1 - NBUF))
                    for q in quadrants:
                        eng.dma_start(raw[c % NBUF][q * S:(q + 1) * S, :, :],
                                      adj_chunk(b, c, q)).then_inc(loaded[c % NBUF], 16)
            over_blocks(eng, body)

        @block.sync
        def _(sp):
            for q in range(Q):
                sp.dma_start(feat[q * S:(q + 1) * S, :, :], stretch(item, q)).then_inc(items_loaded, 16)
            load_adj(sp, 0, (0, 1), low_loaded)
            load_adj(sp, 1, (0, 1), low_loaded)

        @block.gpsimd
        def _(pool):
            nc.gpsimd.memset(ident[:], 0.0).then_inc(ident_zeroed, 1)
            nc.gpsimd.memset(first_named[:], 1.0).then_inc(masks_set, 1)
            pool.wait_ge(ident_zeroed, 1)
            nc.gpsimd.affine_select(out=ident[:], in_=ident[:], compare_op=ALU.not_equal, fill=1.0, base=0,
                                    pattern=[[-1, P]], channel_multiplier=1).then_inc(masks_ready, 1)
            pool.wait_ge(masks_set, 1)
            for q in range(Q - 1):
                pool.wait_ge(masks_ready, q + 1)
                part = first_named[q * S:(q + 1) * S, :]
                nc.gpsimd.affine_select(out=part, in_=part, compare_op=ALU.is_ge, fill=0.0, base=QSTRIDE - 1,
                                        pattern=[[-S, COLBLOCKS]], channel_multiplier=-1).then_inc(masks_ready, 1)
            load_adj(pool, 0, (2, 3), high_loaded)
            load_adj(pool, 1, (2, 3), high_loaded)

        @block.scalar
        def _(act):
            act.dma_start(w_item_nat[:], w_item).then_inc(consts_loaded, 16)
            act.dma_start(w_user_nat[:], w_user).then_inc(consts_loaded, 16)
            act.dma_start(w_msg_sb[:], w_msg).then_inc(consts_loaded, 16)
            act.dma_start(b_item_bc[:], b_item.rearrange("(a d) -> a d", a=1).to_broadcast([P, D])).then_inc(consts_loaded, 16)
            act.dma_start(b_msg_bc[:], b_msg.rearrange("(a d) -> a d", a=1).to_broadcast([P, D])).then_inc(consts_loaded, 16)
            act.dma_start(b_user_col[:], b_user.rearrange("(d a) -> d a", a=1)).then_inc(consts_loaded, 16)
            act.wait_ge(w_transposed, 1)
            nc.scalar.activation(w_item_t[:], p_xt[:, 0:D], ACT.Copy).then_inc(w_copied, 1)
            nc.scalar.activation(w_user_t[:], p_xt[:, D:2 * D], ACT.Copy).then_inc(w_copied, 1)
            for k in range(GROUPS):
                act.wait_ge(item_transposed, k + 1)
                if k >= 2:
                    act.wait_ge(item_product, k - 1)
                nc.scalar.activation((x_t, x1_t)[k % 2][:], (p_xt, p_x1t)[k % 2][:], ACT.Copy).then_inc(item_t_copied, 1)
            act.wait_ge(item_product, GROUPS)
            act.wait_ge(consts_loaded, 6 * 16)
            act.wait_ge(biases_set, 3)

            def sums_out(e, layer, parity):
                ge = e + layer * BLOCKS
                if layer:
                    act.wait_ge(x1_stored, BLOCKS * 16)
                    if is_start(e):
                        act.wait_ge(msg_stored, BLOCKS * 16)
                    else:
                        act.wait_ge(out_stored, e * 16)
                elif not is_start(e):
                    act.wait_ge(x1_stored, e * 16)
                act.dma_start(res[:], block_rows(x1_dram if layer else x, e)).then_inc(res_loaded, 16)
                if layer:
                    act.wait_ge(multiplied, ge * CHUNKS + CHUNKS)
                else:
                    act.wait_ge(sums_done, ge + 1)
                if layer or not is_start(e):
                    act.wait_ge(z_transposed, ge)
                if layer:
                    nc.scalar.activation(z_t[:], acc[(parity + 1) % 2][:], ACT.Copy).then_inc(z_t_ready, 1)
                else:
                    nc.scalar.activation(z_t[:], acc[parity][:], ACT.Relu, bias=b_user_col[:]).then_inc(z_t_ready, 1)

            def rstd_guess(ge):
                act.wait_ge(var_ready, ge + 1)
                nc.scalar.activation(log_var[:], var_eps[:], ACT.Ln).then_inc(log_var_ready, 1)
                act.wait_ge(log_var_ready, ge + 1)
                nc.scalar.activation(rstd0[:], log_var[:], ACT.Exp, scale=-0.5).then_inc(rstd0_ready, 1)

            def load_x(b):
                if not is_start(b):
                    act.wait_ge(x_transposed, b)
                act.dma_start(x_rows[:], block_rows(x, b)).then_inc(x_loaded, 16)

            def x_t_out(b):
                act.wait_ge(x_transposed, b + 1)
                if not is_start(b):
                    act.wait_ge(sums_done, b)
                nc.scalar.activation(x_t[:, 0:BLOCK], p_xt[:, 0:BLOCK], ACT.Copy).then_inc(x_t_ready, 1)

            def x1_out(e):
                act.wait_ge(x1_transposed, e + 1)
                if not is_start(e):
                    act.wait_ge(msg_product, e)
                nc.scalar.activation(x1_t[:, 0:BLOCK], p_x1t[:, 0:BLOCK], ACT.Copy).then_inc(x1_t_ready, 1)
                act.wait_ge(normed, e + 1)
                act.dma_start(block_rows(x1_dram, e), res[:]).then_inc(x1_stored, 16)

            def msg_out(e):
                act.wait_ge(msg_ready, e + 1)
                if not is_start(e):
                    act.wait_ge(msg_stored, e * 16)
                act.dma_start(block_rows(msg_dram, e), msg[:]).then_inc(msg_stored, 16)

            load_x(0)
            x_t_out(0)

            def layer1_after(b, e, parity):
                load_x(b)
                sums_out(e, 0, 1 - parity)
                x_t_out(b)
                rstd_guess(e)
                x1_out(e)
                msg_out(e)

            layer1_after(1, 0, 1)
            layer1_after(2, 1, 0)
            with act.Fori(3, BLOCKS - 1, 2) as b:
                layer1_after(b, b - 1, 1)
                layer1_after(b + 1, b, 0)
            last = BLOCKS - 1
            sums_out(last, 0, last % 2)
            rstd_guess(last)
            x1_out(last)
            msg_out(last)
            act.wait_ge(msg_stored, BLOCKS * 16)
            act.wait_ge(sums_done, BLOCKS)
            for q in range(Q):
                act.dma_start(feat[q * S:(q + 1) * S, :, :], stretch(msg_dram, q)).then_inc(msg_loaded, 16)

            def square_and_weigh(k, c):
                flat = tr[c % NBUF][:, :, :, :]
                if c in DVE_SQUARED:
                    return
                act.wait_ge(inverted, k + 1)
                nc.scalar.activation(flat, flat, ACT.Square, bias=minus1[:]).then_inc(act_squared, 1)

            def weigh(b, k, c):
                flat = tr[c % NBUF][:, :, :, :]
                if c in DVE_SQUARED:
                    act.wait_ge(dve_squared, b * len(DVE_SQUARED) + (DVE_SQUARED.index(c) + 1))
                    nc.scalar.activation(flat, flat, ACT.Exp, bias=minus2[:], scale=-2.0).then_inc(weighted, 1)
                else:
                    own = [i for i in range(CHUNKS) if i not in DVE_SQUARED]
                    act.wait_ge(act_squared, b * len(own) + (own.index(c) + 1))
                    nc.scalar.activation(flat, flat, ACT.Exp, scale=-2.0).then_inc(weighted, 1)

            def store_out(e):
                act.wait_ge(normed, e + (BLOCKS + 1))
                act.dma_start(block_rows(out, e), res[:]).then_inc(out_stored, 16)

            def layer2(b, e, parity):
                for c in range(CHUNKS):
                    k = b * CHUNKS + c
                    flat = tr[c % NBUF][:, :, :, :]
                    act.wait_ge(transposed, k + (BLOCKS * CHUNKS + 1))
                    nc.scalar.activation(flat, flat, ACT.Ln, bias=tiny[:]).then_inc(logged, 1)
                    before = c > 0 or e is not None
                    if before:
                        square_and_weigh(k - 1, (c - 1) % CHUNKS)
                    act.wait_ge(logged, k + 1)
                    nc.scalar.activation(flat, flat, ACT.Exp, scale=-1.0).then_inc(inverted, 1)
                    if before:
                        weigh(b if c else e, k - 1, (c - 1) % CHUNKS)
                    if e is not None:
                        if c == 2:
                            sums_out(e, 1, 1 - parity)
                        if c == 5:
                            rstd_guess(e + BLOCKS)
                        if c == 7:
                            store_out(e)

            layer2(0, None, 0)
            layer2(1, 0, 1)
            layer2(2, 1, 0)
            with act.Fori(3, BLOCKS - 1, 2) as b:
                layer2(b, b - 1, 1)
                layer2(b + 1, b, 0)
            k_last = BLOCKS * CHUNKS - 1
            square_and_weigh(k_last, CHUNKS - 1)
            weigh(last, k_last, CHUNKS - 1)
            sums_out(last, 1, last % 2)
            rstd_guess(last + BLOCKS)
            store_out(last)
            act.wait_ge(out_stored, BLOCKS * 16)

        @block.vector
        def _(dve):
            nc.vector.memset(tiny[:], TINY).then_inc(biases_set, 1)
            nc.vector.memset(minus1[:], -1.0).then_inc(biases_set, 1)
            nc.vector.memset(minus2[:], -2.0).then_inc(biases_set, 1)
            dve.wait_ge(consts_loaded, 6 * 16)
            for k in range(GROUPS):
                dve.wait_ge(item_product, k + 1)
                for j in range(SUB):
                    last = nc.vector.tensor_tensor(feat[:, k * SUB + j, :], (p_z, p_msg)[k % 2][:, j, :], b_item_bc[:], ALU.add)
                last.then_inc(item_features, 1)
            dve.wait_ge(masks_ready, Q)
            dve.wait_ge(item_features, GROUPS)

            def clear_duplicates(signal):
                for j in range(FIRST_DUP, COLBLOCKS):
                    nc.vector.tensor_scalar(feat[:, j, :], feat[:, j, :], first_named[:, j:j + 1], None, ALU.mult).then_inc(signal, 1)

            clear_duplicates(features_ready)

            def transpose_chunk(g, c, start):
                if not start or c >= NBUF:
                    dve.wait_ge(multiplied, g * CHUNKS + (c + 1 - NBUF))
                nc.vector.transpose(tr[c % NBUF][:, :, :, :].rearrange("p r j s -> p (r j s)"),
                                    raw[c % NBUF][:, :, :].rearrange("p r n -> p (r n)")).then_inc(transposed, 1)

            STEPS = 5

            def add_and_stats(ge, first_ever):
                dve.wait_ge(res_loaded, ge * 16 + 16)
                dve.wait_ge(z_transposed, ge + 1)
                nc.vector.tensor_tensor(res[:], res[:], p_z[0:SP_ROWS, :, :], ALU.add).then_inc(res_added, 1)
                dve.wait_ge(res_added, ge + 1)
                for s in range(SUB):
                    last = nc.vector.bn_stats(stats[:, s, :], res[:, s, :])
                last.then_inc(norm_step, 1)
                dve.wait_ge(norm_step, ge * STEPS + 1)
                nc.vector.memset(var_eps[:], EPS)
                for s in range(SUB):
                    last = nc.vector.bn_aggr(meanvar[:, s, :], stats[:, s, :])
                last.then_inc(norm_step, 1)
                dve.wait_ge(norm_step, ge * STEPS + 2)
                nc.vector.tensor_tensor(var_eps[:], var_eps[:], meanvar[:, :, 1], ALU.add).then_inc(var_ready, 1)

            def normalise(ge):
                dve.wait_ge(rstd0_ready, ge + 1)
                nc.vector.tensor_tensor(newton[:], rstd0[:], rstd0[:], ALU.mult).then_inc(norm_step, 1)
                dve.wait_ge(norm_step, ge * STEPS + 3)
                nc.vector.tensor_tensor(newton[:], newton[:], var_eps[:], ALU.mult).then_inc(norm_step, 1)
                dve.wait_ge(norm_step, ge * STEPS + 4)
                nc.vector.tensor_scalar(newton[:], newton[:], -0.5, 1.5, ALU.mult, ALU.add).then_inc(norm_step, 1)
                dve.wait_ge(norm_step, ge * STEPS + 5)
                nc.vector.tensor_tensor(rstd[:], newton[:], rstd0[:], ALU.mult).then_inc(rstd_refined, 1)
                dve.wait_ge(rstd_refined, ge + 1)
                for s in range(SUB):
                    last = nc.vector.tensor_scalar(res[:, s, :], res[:, s, :], meanvar[:, s, 0:1], rstd[:, s:s + 1],
                                                   ALU.subtract, ALU.mult)
                last.then_inc(normed, 1)

            def msg_bias(e, start):
                dve.wait_ge(msg_product, e + 1)
                if not start:
                    dve.wait_ge(msg_stored, e * 16)
                for s in range(SUB):
                    last = nc.vector.tensor_tensor(msg[:, s, :], p_msg[0:SP_ROWS, s, :], b_msg_bc[0:SP_ROWS, :], ALU.add)
                last.then_inc(msg_ready, 1)

            def layer1(b, e, start, e_start):
                for c in range(CHUNKS):
                    dve.wait_ge(low_loaded[c % NBUF], (b * USES + (c // NBUF + 1)) * (Q // 2 * 16))
                    dve.wait_ge(high_loaded[c % NBUF], (b * USES + (c // NBUF + 1)) * (Q // 2 * 16))
                    transpose_chunk(b, c, start)
                    if e is not None:
                        if c == 4:
                            add_and_stats(e, e_start)
                        if c == 5:
                            normalise(e)
                        if c == 7:
                            msg_bias(e, e_start)

            layer1(0, None, True, False)
            layer1(1, 0, False, True)
            layer1(2, 1, False, False)
            with dve.Fori(3, BLOCKS - 1, 2) as b:
                layer1(b, b - 1, False, False)
                layer1(b + 1, b, False, False)
            last_block = BLOCKS - 1
            add_and_stats(last_block, False)
            normalise(last_block)
            msg_bias(last_block, False)

            def square(b, c):
                flat = tr[c % NBUF][:, :, :, :].rearrange("p r j s -> p (r j s)")
                dve.wait_ge(inverted, b * CHUNKS + (c + 1))
                nc.vector.scalar_tensor_tensor(flat, flat, 2.0, flat, ALU.subtract, ALU.mult).then_inc(dve_squared, 1)

            def layer2(b, e):
                g = b + BLOCKS
                for c in range(CHUNKS):
                    flat = raw[c % NBUF][:, :, :].rearrange("p r n -> p (r n)")
                    dve.wait_ge(low_loaded[c % NBUF], (g * USES + (c // NBUF + 1)) * (Q // 2 * 16))
                    dve.wait_ge(high_loaded[c % NBUF], (g * USES + (c // NBUF + 1)) * (Q // 2 * 16))
                    nc.vector.scalar_tensor_tensor(flat, flat, 1.0, flat, ALU.is_lt, ALU.mult).then_inc(masked, 1)
                    if c - 2 in DVE_SQUARED:
                        square(b, c - 2)
                    dve.wait_ge(masked, b * CHUNKS + (c + 1))
                    transpose_chunk(g, c, False)
                    if e is None and c == 4:
                        dve.wait_ge(msg_loaded, Q * 16)
                        clear_duplicates(msg_masked)
                    if e is not None:
                        if c == 5:
                            add_and_stats(e + BLOCKS, False)
                        if c == 7:
                            normalise(e + BLOCKS)

            layer2(0, None)
            with dve.Fori(1, BLOCKS - 1, 2) as b:
                layer2(b, b - 1)
                layer2(b + 1, b)
            add_and_stats(last_block + BLOCKS, False)
            normalise(last_block + BLOCKS)

        @block.tensor
        def _(pe):
            pe.wait_ge(consts_loaded, 6 * 16)
            pe.wait_ge(masks_ready, Q)
            nc.tensor.transpose(p_xt[:, 0:D], w_item_nat[:], ident[:])
            nc.tensor.transpose(p_xt[:, D:2 * D], w_user_nat[:], ident[:]).then_inc(w_transposed, 1)
            pe.wait_ge(w_copied, 2)
            pe.wait_ge(items_loaded, Q * 16)

            def item_transposes(k):
                if k >= 2:
                    pe.wait_ge(item_t_copied, k - 1)
                for j in range(SUB):
                    last = nc.tensor.transpose((p_xt, p_x1t)[k % 2][:, j * P:(j + 1) * P], feat[:, k * SUB + j, :], ident[:])
                last.then_inc(item_transposed, 1)

            item_transposes(0)
            for k in range(GROUPS):
                if k + 1 < GROUPS:
                    item_transposes(k + 1)
                pe.wait_ge(item_t_copied, k + 1)
                if k >= 2:
                    pe.wait_ge(item_features, k - 1)
                for j in range(SUB):
                    last = nc.tensor.matmul((p_z, p_msg)[k % 2][:, j, :], (x_t, x1_t)[k % 2][:, j * P:(j + 1) * P], w_item_t[:],
                                            start=True, stop=True)
                last.then_inc(item_product, 1)
            pe.wait_ge(features_ready, DUPS)

            def chunk_products(parity, c, last_of_block):
                for j in range(CB):
                    jj = c * CB + j
                    last = nc.tensor.matmul(acc[parity][:], feat[:, jj, :], tr[c % NBUF][:, :, j, :],
                                            start=(jj == 0), stop=(last_of_block and jj == COLBLOCKS - 1))
                return last

            def z_transposes(ge, start):
                pe.wait_ge(z_t_ready, ge + 1)
                if not start:
                    pe.wait_ge(res_added, ge)
                for s in range(SUB):
                    last = nc.tensor.transpose(p_z[0:SP_ROWS, s, :], z_t[:, s * SP_ROWS:(s + 1) * SP_ROWS], ident[:])
                last.then_inc(z_transposed, 1)

            def x_transposes(b, start):
                pe.wait_ge(x_loaded, b * 16 + 16)
                if not start:
                    pe.wait_ge(x_t_ready, b)
                for s in range(SUB):
                    last = nc.tensor.transpose(p_xt[:, s * SP_ROWS:(s + 1) * SP_ROWS], x_rows[:, s, :],
                                               ident[0:SP_ROWS, 0:SP_ROWS])
                last.then_inc(x_transposed, 1)

            def x1_transposes(e, start):
                pe.wait_ge(normed, e + 1)
                if not start:
                    pe.wait_ge(x1_t_ready, e)
                for s in range(SUB):
                    last = nc.tensor.transpose(p_x1t[:, s * SP_ROWS:(s + 1) * SP_ROWS], res[:, s, :],
                                               ident[0:SP_ROWS, 0:SP_ROWS])
                last.then_inc(x1_transposed, 1)

            def msg_products(e, start):
                pe.wait_ge(x1_t_ready, e + 1)
                if not start:
                    pe.wait_ge(msg_ready, e)
                for s in range(SUB):
                    last = nc.tensor.matmul(p_msg[0:SP_ROWS, s, :], x1_t[:, s * SP_ROWS:(s + 1) * SP_ROWS], w_msg_sb[:],
                                            start=True, stop=True)
                last.then_inc(msg_product, 1)

            def layer1(b, e, parity, e_start):
                if e is not None and not e_start:
                    pe.wait_ge(z_t_ready, b - 1)
                for c in range(CHUNKS):
                    pe.wait_ge(transposed, b * CHUNKS + (c + 1))
                    chunk_products(parity, c, False).then_inc(multiplied, 1)
                    if c == 1:
                        x_transposes(b, e is None)
                    if e is not None:
                        if c == 0:
                            z_transposes(e, e_start)
                        if c == 3:
                            x1_transposes(e, e_start)
                        if c == 4:
                            msg_products(e, e_start)
                pe.wait_ge(x_t_ready, b + 1)
                nc.tensor.matmul(acc[parity][:], w_user_t[:], x_t[:, 0:BLOCK], start=False, stop=True).then_inc(sums_done, 1)

            layer1(0, None, 0, False)
            layer1(1, 0, 1, True)
            layer1(2, 1, 0, False)
            with pe.Fori(3, BLOCKS - 1, 2) as b:
                layer1(b, b - 1, 1, False)
                layer1(b + 1, b, 0, False)
            last_block = BLOCKS - 1
            z_transposes(last_block, False)
            x1_transposes(last_block, False)
            msg_products(last_block, False)

            pe.wait_ge(msg_loaded, Q * 16)

            def layer2(b, e, parity):
                g = b + BLOCKS
                pe.wait_ge(z_t_ready, g - 1)
                for c in range(CHUNKS):
                    pe.wait_ge(weighted, b * CHUNKS + (c + 1))
                    if e is None and c == CHUNKS - 1:
                        pe.wait_ge(msg_masked, DUPS)
                    last = chunk_products(parity, c, True)
                    last.then_inc(multiplied, 1)
                    if e is not None and c == 1:
                        z_transposes(e + BLOCKS, False)

            layer2(0, None, 1)
            with pe.Fori(1, BLOCKS - 1, 2) as b:
                layer2(b, b - 1, 0)
                layer2(b + 1, b, 1)
            z_transposes(last_block + BLOCKS, False)


_INS = ['x', 'adj', 'L0_gnn_item_feat', 'L0_gnn_W_item', 'L0_gnn_b_item', 'L0_gnn_W_user', 'L0_gnn_b_user',
        'L1_gnn_W', 'L1_gnn_B']
_OUTS = [((10000, 128), 'float32')]


def kernel(**inputs):
    import numpy as _np
    import concourse.bacc as _bacc
    from concourse import mybir as _mybir
    from concourse.bass_utils import run_bass_kernel_spmd as _run

    nc = _bacc.Bacc("TRN2", target_bir_lowering=False, num_devices=1)
    arrays, args = {}, []
    for name in _INS:
        a = _np.ascontiguousarray(inputs[name])
        arrays[f"in_{name}_dram"] = a
        args.append(nc.dram_tensor(f"in_{name}_dram", a.shape, _mybir.dt.from_np(a.dtype), kind="ExternalInput").ap())
    for i, (shape, dtype) in enumerate(_OUTS):
        dt = _mybir.dt.from_np(_np.dtype(dtype))
        args.append(nc.dram_tensor(f"out_{i}_dram", shape, dt, kind="ExternalOutput").ap())
    two_graph_layers(nc, *args)
    r = _run(nc, [arrays], core_ids=[0])
    return r.results[0]["out_0_dram"]
```

```python
import numpy as np
from contextlib import ExitStack

import concourse.bass as bass
from concourse import mybir


def two_graph_layers(nc, x, adj, item, w_item, b_item, w_user, b_user, w_msg, b_msg, out):
    F32 = mybir.dt.float32
    ALU = mybir.AluOpType
    ACT = mybir.ActivationFunctionType

    N, D = x.shape
    P = 128
    S = 32
    Q = P // S
    COLBLOCKS = 80
    QCOLS = COLBLOCKS * S
    QSTRIDE = (N - QCOLS) // (Q - 1)
    assert QSTRIDE * (Q - 1) + QCOLS == N and QSTRIDE <= QCOLS
    CHUNKS = 10
    CB = COLBLOCKS // CHUNKS
    CCOLS = CB * S
    RG = 15
    BLOCK = RG * S
    BLOCKS = 21
    BSTRIDE = (N - BLOCK) // (BLOCKS - 1)
    assert BSTRIDE * (BLOCKS - 1) + BLOCK == N and BSTRIDE <= BLOCK
    SUB = 4
    SP_ROWS = BLOCK // SUB
    CHUNK = RG * CCOLS
    EARLY = [1, 3, 5, 7]
    LATE = [c for c in range(CHUNKS) if c not in EARLY]
    NE, NL = len(EARLY), len(LATE)
    PAIRS = NL // 2
    AFTER_PAIR = [[0], [1, 2], [3]]
    assert len(AFTER_PAIR) == PAIRS and sorted(sum(AFTER_PAIR, [])) == list(range(NE)) and 2 * PAIRS == NL
    RAW1, TR1, EARLY1 = 5, 2, 2
    RAW2, EARLY2, TR2 = 4, 2, 4
    NBUF = max(RAW1 + TR1 + EARLY1, RAW2 + EARLY2 + TR2)
    EPS = 1e-5
    TINY = 2.0 ** -60
    FIRST_DUP = QSTRIDE // S
    DUPS = COLBLOCKS - FIRST_DUP
    GROUPS = COLBLOCKS // SUB

    x1_dram = nc.dram_tensor("x1_scratch", (N, D), F32, kind="Internal").ap()
    early_dram = nc.dram_tensor("early_weights", (BLOCKS * NE * P, CHUNK), F32, kind="Internal").ap()
    msg_dram = nc.dram_tensor("msg_scratch", (N, D), F32, kind="Internal").ap()

    def block_rows(dram, b):
        return dram[bass.ds(b * BSTRIDE, BLOCK), :].rearrange("(q p) d -> p q d", p=SP_ROWS)

    def stretch(dram, q):
        return dram[q * QSTRIDE:q * QSTRIDE + QCOLS, :].rearrange("(j p) d -> p j d", p=S)

    def chunk_cols(c, q):
        return min(CCOLS, QSTRIDE - c * CCOLS) if q < Q - 1 else CCOLS

    def adj_chunk(b, c, q):
        rows = adj[bass.ds(b * BSTRIDE, BLOCK), :].rearrange("(r p) n -> p r n", p=S)
        return rows[:, :, q * QSTRIDE + c * CCOLS:q * QSTRIDE + c * CCOLS + chunk_cols(c, q)]

    def slot(parity, i, per_block, ring):
        assert 2 * per_block % ring == 0
        return (parity * per_block + i) % ring

    def early_weights(b, i):
        return early_dram[bass.ds(b * (NE * P) + i * P, P), :]

    ctx = ExitStack()
    with ctx:
        def sb(name, shape):
            return ctx.enter_context(nc.sbuf_tensor(name, shape, F32))

        def ps(name, shape):
            return ctx.enter_context(nc.psum_tensor(name, shape, F32))

        def sem(name):
            return ctx.enter_context(nc.semaphore(name))

        feat = sb("feat", [P, COLBLOCKS, D])
        chunks = [sb(f"chunk{i}", [P, CHUNK]) for i in range(NBUF)]
        raw1, tr1, early1 = chunks[0:RAW1], chunks[RAW1:RAW1 + TR1], chunks[RAW1 + TR1:RAW1 + TR1 + EARLY1]
        raw2, early2, tr2 = chunks[0:RAW2], chunks[RAW2:RAW2 + EARLY2], chunks[RAW2 + EARLY2:RAW2 + EARLY2 + TR2]
        ident = sb("ident", [P, P])
        first_named = sb("first_named", [P, COLBLOCKS])
        w_item_t = sb("w_item_t", [D, D])
        w_user_t = sb("w_user_t", [D, D])
        w_msg_sb = sb("w_msg_sb", [D, D])
        b_item_bc = sb("b_item_bc", [P, D])
        b_msg_bc = sb("b_msg_bc", [P, D])
        b_user_col = sb("b_user_col", [D, 1])
        tiny = sb("tiny", [P, 1])
        minus1 = sb("minus1", [P, 1])
        minus2 = sb("minus2", [P, 1])
        x_rows = [sb(f"x_rows{i}", [SP_ROWS, SUB, D]) for i in range(2)]
        x_t = sb("x_t", [D, SUB * P])
        z_t = sb("z_t", [D, BLOCK])
        w_item_nat, w_user_nat = z_t[:, 0:D], z_t[:, D:2 * D]
        res = sb("res", [SP_ROWS, SUB, D])
        x1_t = sb("x1_t", [D, SUB * P])
        msg = sb("msg", [SP_ROWS, SUB, D])
        stats = sb("stats", [SP_ROWS, SUB, 6])
        meanvar = sb("meanvar", [SP_ROWS, SUB, 2])
        var_eps = sb("var_eps", [SP_ROWS, SUB])
        log_var = sb("log_var", [SP_ROWS, SUB])
        rstd0 = sb("rstd0", [SP_ROWS, SUB])
        newton = sb("newton", [SP_ROWS, SUB])
        rstd = sb("rstd", [SP_ROWS, SUB])

        acc = [ps(f"acc{i}", [D, BLOCK]) for i in range(2)]
        p_xt = ps("p_xt", [D, SUB * P])
        p_z = ps("p_z", [P, SUB, D])
        p_x1t = ps("p_x1t", [D, SUB * P])
        p_msg = ps("p_msg", [P, SUB, D])

        consts_loaded = sem("consts_loaded")
        items_loaded = sem("items_loaded")
        ident_zeroed = sem("ident_zeroed")
        biases_set = sem("biases_set")
        masks_set = sem("masks_set")
        masks_ready = sem("masks_ready")
        w_transposed = sem("w_transposed")
        w_copied = sem("w_copied")
        item_transposed = sem("item_transposed")
        item_t_copied = sem("item_t_copied")
        item_product = sem("item_product")
        item_features = sem("item_features")
        features_ready = sem("features_ready")
        low_loaded = [sem(f"low_loaded{i}") for i in range(RAW1)]
        high_loaded = [sem(f"high_loaded{i}") for i in range(RAW1)]
        late_low_loaded = [sem(f"late_low_loaded{i}") for i in range(RAW2)]
        late_high_loaded = [sem(f"late_high_loaded{i}") for i in range(RAW2)]
        transposed = sem("transposed")
        multiplied = sem("multiplied")
        early_masked = sem("early_masked")
        early_stored = [sem(f"early_stored{i}") for i in range(EARLY1)]
        masked = sem("masked")
        late_transposed = sem("late_transposed")
        late_multiplied = sem("late_multiplied")
        early_loaded = [sem(f"early_loaded{i}") for i in range(EARLY2)]
        early_multiplied = sem("early_multiplied")
        logged = sem("logged")
        inverted = sem("inverted")
        squared = sem("squared")
        dve_squared = sem("dve_squared")
        weighted = sem("weighted")
        x_loaded = [sem(f"x_loaded{i}") for i in range(2)]
        x_transposed = sem("x_transposed")
        x_t_ready = sem("x_t_ready")
        sums_done = sem("sums_done")
        z_t_ready = sem("z_t_ready")
        z_transposed = sem("z_transposed")
        res_loaded = sem("res_loaded")
        res_added = sem("res_added")
        norm_step = sem("norm_step")
        var_ready = sem("var_ready")
        log_var_ready = sem("log_var_ready")
        rstd0_ready = sem("rstd0_ready")
        rstd_refined = sem("rstd_refined")
        normed = sem("normed")
        x1_transposed = sem("x1_transposed")
        x1_t_ready = sem("x1_t_ready")
        msg_product = sem("msg_product")
        msg_ready = sem("msg_ready")
        x1_stored = sem("x1_stored")
        msg_stored = sem("msg_stored")
        msg_loaded = sem("msg_loaded")
        msg_masked = sem("msg_masked")
        out_stored = sem("out_stored")

        block = ctx.enter_context(nc.Block())

        def over_blocks(eng, body):
            body(0, 0)
            with eng.Fori(1, BLOCKS - 1, 2) as b:
                body(b, 1)
                body(b + 1, 0)

        def is_start(b):
            return isinstance(b, int) and b == 0

        def last_use(ring, at, of_all):
            return of_all - (of_all - 1 - at) % ring

        def wait_layer1(eng, buffer):
            n = chunks.index(buffer)
            if n < RAW1:
                eng.wait_ge(transposed, last_use(RAW1, n, BLOCKS * CHUNKS))
            elif n < RAW1 + TR1:
                eng.wait_ge(multiplied, last_use(TR1, n - RAW1, BLOCKS * CHUNKS))
            elif n < RAW1 + TR1 + EARLY1:
                eng.wait_ge(early_stored[n - RAW1 - TR1], BLOCKS * NE // EARLY1 * 16)

        def load_adj(eng, buffer, b, c, quadrants, loaded):
            view = buffer[:].rearrange("p (r n) -> p r n", r=RG)
            for q in quadrants:
                eng.dma_start(view[q * S:(q + 1) * S, :, 0:chunk_cols(c, q)], adj_chunk(b, c, q)).then_inc(loaded, 16)

        def load_all_adj(eng, quadrants, loaded, late_loaded):
            def layer1(b, parity):
                for c in range(CHUNKS):
                    if not is_start(b) or c >= RAW1:
                        eng.wait_ge(transposed, b * CHUNKS + (c + 1 - RAW1))
                    at = slot(parity, c, CHUNKS, RAW1)
                    load_adj(eng, raw1[at], b, c, quadrants, loaded[at])

            def layer2(b, parity):
                for i, c in enumerate(LATE):
                    at = slot(parity, i, NL, RAW2)
                    if is_start(b) and i < RAW2:
                        wait_layer1(eng, raw2[at])
                    else:
                        eng.wait_ge(late_transposed, b * NL + (i + 1 - RAW2))
                    load_adj(eng, raw2[at], b, c, quadrants, late_loaded[at])

            over_blocks(eng, layer1)
            over_blocks(eng, layer2)

        @block.sync
        def _(sp):
            for q in range(Q):
                sp.dma_start(feat[q * S:(q + 1) * S, :, :], stretch(item, q)).then_inc(items_loaded, 16)
            load_all_adj(sp, (0, 1), low_loaded, late_low_loaded)

        @block.gpsimd
        def _(pool):
            nc.gpsimd.memset(ident[:], 0.0).then_inc(ident_zeroed, 1)
            nc.gpsimd.memset(first_named[:], 1.0).then_inc(masks_set, 1)
            pool.wait_ge(ident_zeroed, 1)
            nc.gpsimd.affine_select(out=ident[:], in_=ident[:], compare_op=ALU.not_equal, fill=1.0, base=0,
                                    pattern=[[-1, P]], channel_multiplier=1).then_inc(masks_ready, 1)
            pool.wait_ge(masks_set, 1)
            for q in range(Q - 1):
                pool.wait_ge(masks_ready, q + 1)
                part = first_named[q * S:(q + 1) * S, :]
                nc.gpsimd.affine_select(out=part, in_=part, compare_op=ALU.is_ge, fill=0.0, base=QSTRIDE - 1,
                                        pattern=[[-S, COLBLOCKS]], channel_multiplier=-1).then_inc(masks_ready, 1)
            load_all_adj(pool, (2, 3), high_loaded, late_high_loaded)

        @block.scalar
        def _(act):
            nc.scalar.preload_act_table_set("natural_log_exp_and_others")
            act.dma_start(w_item_nat, w_item).then_inc(consts_loaded, 16)
            act.dma_start(w_user_nat, w_user).then_inc(consts_loaded, 16)
            act.dma_start(w_msg_sb[:], w_msg).then_inc(consts_loaded, 16)
            act.dma_start(b_item_bc[:], b_item.rearrange("(a d) -> a d", a=1).to_broadcast([P, D])).then_inc(consts_loaded, 16)
            act.dma_start(b_msg_bc[:], b_msg.rearrange("(a d) -> a d", a=1).to_broadcast([P, D])).then_inc(consts_loaded, 16)
            act.dma_start(b_user_col[:], b_user.rearrange("(d a) -> d a", a=1)).then_inc(consts_loaded, 16)
            act.wait_ge(w_transposed, 1)
            nc.scalar.activation(w_item_t[:], p_xt[:, 0:D], ACT.Copy).then_inc(w_copied, 1)
            nc.scalar.activation(w_user_t[:], p_xt[:, D:2 * D], ACT.Copy).then_inc(w_copied, 1)
            for k in range(GROUPS):
                act.wait_ge(item_transposed, k + 1)
                if k >= 2:
                    act.wait_ge(item_product, k - 1)
                nc.scalar.activation((x_t, x1_t)[k % 2][:], (p_xt, p_x1t)[k % 2][:], ACT.Copy).then_inc(item_t_copied, 1)
            act.wait_ge(item_product, GROUPS)
            act.wait_ge(consts_loaded, 6 * 16)
            act.wait_ge(biases_set, 3)

            def sums_out(e, layer, parity):
                ge = e + layer * BLOCKS
                if layer:
                    act.wait_ge(x1_stored, BLOCKS * 16)
                    if not is_start(e):
                        act.wait_ge(out_stored, e * 16)
                    act.dma_start(res[:], block_rows(x1_dram, e)).then_inc(res_loaded, 16)
                    act.wait_ge(late_multiplied, e * NL + NL)
                else:
                    act.wait_ge(sums_done, ge + 1)
                if layer or not is_start(e):
                    act.wait_ge(z_transposed, ge)
                if layer:
                    nc.scalar.activation(z_t[:], acc[(parity + BLOCKS) % 2][:], ACT.Copy).then_inc(z_t_ready, 1)
                else:
                    nc.scalar.activation(z_t[:], acc[parity][:], ACT.Relu, bias=b_user_col[:]).then_inc(z_t_ready, 1)

            def rstd_guess(ge):
                act.wait_ge(var_ready, ge + 1)
                nc.scalar.activation(log_var[:], var_eps[:], ACT.Ln).then_inc(log_var_ready, 1)
                act.wait_ge(log_var_ready, ge + 1)
                nc.scalar.activation(rstd0[:], log_var[:], ACT.Exp, scale=-0.5).then_inc(rstd0_ready, 1)

            def load_x(b, parity, second):
                if not is_start(b) and not second:
                    act.wait_ge(res_added, b - 1)
                act.dma_start(x_rows[parity][:], block_rows(x, b)).then_inc(x_loaded[parity], 16)

            def x_t_out(b):
                act.wait_ge(x_transposed, b + 1)
                if not is_start(b):
                    act.wait_ge(sums_done, b)
                nc.scalar.activation(x_t[:, 0:BLOCK], p_xt[:, 0:BLOCK], ACT.Copy).then_inc(x_t_ready, 1)

            def x1_out(e):
                act.wait_ge(x1_transposed, e + 1)
                if not is_start(e):
                    act.wait_ge(msg_product, e)
                nc.scalar.activation(x1_t[:, 0:BLOCK], p_x1t[:, 0:BLOCK], ACT.Copy).then_inc(x1_t_ready, 1)
                act.wait_ge(normed, e + 1)
                act.dma_start(block_rows(x1_dram, e), res[:]).then_inc(x1_stored, 16)

            def msg_out(e):
                act.wait_ge(msg_ready, e + 1)
                if not is_start(e):
                    act.wait_ge(msg_stored, e * 16)
                act.dma_start(block_rows(msg_dram, e), msg[:]).then_inc(msg_stored, 16)

            def log(buffer):
                nc.scalar.activation(buffer[:], buffer[:], ACT.Ln, bias=TINY).then_inc(logged, 1)

            def invert(buffer, nth):
                act.wait_ge(logged, nth)
                nc.scalar.activation(buffer[:], buffer[:], ACT.Exp, scale=-1.0).then_inc(inverted, 1)

            def square(buffer, nth):
                act.wait_ge(inverted, nth)
                nc.scalar.activation(buffer[:], buffer[:], ACT.Square, bias=-1.0).then_inc(squared, 1)

            def weigh(buffer, nth):
                act.wait_ge(squared, nth)
                nc.scalar.activation(buffer[:], buffer[:], ACT.Exp, scale=-2.0).then_inc(weighted, 1)

            def early_chunk(b, i):
                buffer = early1[i % EARLY1]
                nth = b * NE + (i + 1)
                act.wait_ge(early_masked, nth)
                log(buffer)
                invert(buffer, nth)
                square(buffer, nth)
                weigh(buffer, nth)
                act.wait_ge(weighted, nth)
                act.dma_start(early_weights(b, i), buffer[:]).then_inc(early_stored[i % EARLY1], 16)

            def layer1(b, e, parity):
                load_x(b, parity, is_start(e) if e is not None else False)
                if e is not None:
                    sums_out(e, 0, 1 - parity)
                x_t_out(b)
                if e is not None:
                    rstd_guess(e)
                early_chunk(b, 0)
                early_chunk(b, 1)
                if e is not None:
                    x1_out(e)
                early_chunk(b, 2)
                early_chunk(b, 3)
                if e is not None:
                    msg_out(e)

            layer1(0, None, 0)
            layer1(1, 0, 1)
            layer1(2, 1, 0)
            with act.Fori(3, BLOCKS - 1, 2) as b:
                layer1(b, b - 1, 1)
                layer1(b + 1, b, 0)
            last = BLOCKS - 1

            def load_early(b, i):
                at = i % EARLY2
                if is_start(b) and i < EARLY2:
                    wait_layer1(act, early2[at])
                else:
                    act.wait_ge(early_multiplied, b * NE + (i + 1 - EARLY2))
                act.dma_start(early2[at][:], early_weights(b, i)).then_inc(early_loaded[at], 16)

            for i in range(EARLY1):
                act.wait_ge(early_stored[i], BLOCKS * NE // EARLY1 * 16)
            for i in range(EARLY2):
                load_early(0, i)
            sums_out(last, 0, last % 2)
            rstd_guess(last)
            x1_out(last)
            msg_out(last)
            act.wait_ge(msg_stored, BLOCKS * 16)
            act.wait_ge(sums_done, BLOCKS)
            for q in range(Q):
                act.dma_start(feat[q * S:(q + 1) * S, :, :], stretch(msg_dram, q)).then_inc(msg_loaded, 16)

            def store_out(e):
                act.wait_ge(normed, e + (BLOCKS + 1))
                act.dma_start(block_rows(out, e), res[:]).then_inc(out_stored, 16)

            def layer2(b, e, parity):
                for pair in range(PAIRS):
                    k = b * NL + 2 * pair
                    nth = k + BLOCKS * NE
                    one, two = (tr2[slot(parity, 2 * pair + i, NL, TR2)] for i in range(2))
                    if e is not None and pair == 2:
                        rstd_guess(e + BLOCKS)
                    act.wait_ge(late_transposed, k + 1)
                    log(one)
                    invert(one, nth + 1)
                    act.wait_ge(late_transposed, k + 2)
                    log(two)
                    invert(two, nth + 2)
                    if pair == 0 and not is_start(b):
                        load_early(b, 0)
                    square(two, nth + 2)
                    act.wait_ge(dve_squared, b * PAIRS + (pair + 1))
                    nc.scalar.activation(one[:], one[:], ACT.Exp, bias=-2.0, scale=-2.0).then_inc(weighted, 1)
                    weigh(two, b * PAIRS + (BLOCKS * NE + pair + 1))
                    if pair == 0:
                        if e is not None:
                            sums_out(e, 1, 1 - parity)
                        if not is_start(b):
                            load_early(b, 1)
                    if pair == 1:
                        load_early(b, 2)
                    if pair == 2:
                        load_early(b, 3)
                        if e is not None:
                            store_out(e)

            layer2(0, None, 0)
            layer2(1, 0, 1)
            layer2(2, 1, 0)
            with act.Fori(3, BLOCKS - 1, 2) as b:
                layer2(b, b - 1, 1)
                layer2(b + 1, b, 0)
            sums_out(last, 1, last % 2)
            rstd_guess(last + BLOCKS)
            store_out(last)
            act.wait_ge(out_stored, BLOCKS * 16)

        @block.vector
        def _(dve):
            USES = CHUNKS // RAW1
            assert CHUNKS % RAW1 == 0 and CHUNKS % TR1 == 0 and NE % EARLY1 == 0 and NE % EARLY2 == 0
            nc.vector.memset(tiny[:], TINY).then_inc(biases_set, 1)
            nc.vector.memset(minus1[:], -1.0).then_inc(biases_set, 1)
            nc.vector.memset(minus2[:], -2.0).then_inc(biases_set, 1)
            dve.wait_ge(consts_loaded, 6 * 16)
            for k in range(GROUPS):
                dve.wait_ge(item_product, k + 1)
                for j in range(SUB):
                    last = nc.vector.tensor_tensor(feat[:, k * SUB + j, :], (p_z, p_msg)[k % 2][:, j, :], b_item_bc[:], ALU.add)
                last.then_inc(item_features, 1)
            dve.wait_ge(masks_ready, Q)
            dve.wait_ge(item_features, GROUPS)

            def clear_duplicates(signal):
                for j in range(FIRST_DUP, COLBLOCKS):
                    nc.vector.tensor_scalar(feat[:, j, :], feat[:, j, :], first_named[:, j:j + 1], None, ALU.mult).then_inc(signal, 1)

            clear_duplicates(features_ready)

            STEPS = 5

            def add_and_stats(e, layer, parity, start):
                ge = e + layer * BLOCKS
                if layer:
                    dve.wait_ge(res_loaded, e * 16 + 16)
                elif not start:
                    dve.wait_ge(x1_stored, e * 16)
                dve.wait_ge(z_transposed, ge + 1)
                nc.vector.tensor_tensor(res[:], res[:] if layer else x_rows[parity][:], p_z[0:SP_ROWS, :, :],
                                        ALU.add).then_inc(res_added, 1)
                dve.wait_ge(res_added, ge + 1)
                for s in range(SUB):
                    last = nc.vector.bn_stats(stats[:, s, :], res[:, s, :])
                last.then_inc(norm_step, 1)
                dve.wait_ge(norm_step, ge * STEPS + 1)
                nc.vector.memset(var_eps[:], EPS)
                for s in range(SUB):
                    last = nc.vector.bn_aggr(meanvar[:, s, :], stats[:, s, :])
                last.then_inc(norm_step, 1)
                dve.wait_ge(norm_step, ge * STEPS + 2)
                nc.vector.tensor_tensor(var_eps[:], var_eps[:], meanvar[:, :, 1], ALU.add).then_inc(var_ready, 1)

            def normalise(ge):
                dve.wait_ge(rstd0_ready, ge + 1)
                nc.vector.tensor_tensor(newton[:], rstd0[:], rstd0[:], ALU.mult).then_inc(norm_step, 1)
                dve.wait_ge(norm_step, ge * STEPS + 3)
                nc.vector.tensor_tensor(newton[:], newton[:], var_eps[:], ALU.mult).then_inc(norm_step, 1)
                dve.wait_ge(norm_step, ge * STEPS + 4)
                nc.vector.tensor_scalar(newton[:], newton[:], -0.5, 1.5, ALU.mult, ALU.add).then_inc(norm_step, 1)
                dve.wait_ge(norm_step, ge * STEPS + 5)
                nc.vector.tensor_tensor(rstd[:], newton[:], rstd0[:], ALU.mult).then_inc(rstd_refined, 1)
                dve.wait_ge(rstd_refined, ge + 1)
                for s in range(SUB):
                    last = nc.vector.tensor_scalar(res[:, s, :], res[:, s, :], meanvar[:, s, 0:1], rstd[:, s:s + 1],
                                                   ALU.subtract, ALU.mult)
                last.then_inc(normed, 1)

            def msg_bias(e, start):
                dve.wait_ge(msg_product, e + 1)
                if not start:
                    dve.wait_ge(msg_stored, e * 16)
                for s in range(SUB):
                    last = nc.vector.tensor_tensor(msg[:, s, :], p_msg[0:SP_ROWS, s, :], b_msg_bc[0:SP_ROWS, :], ALU.add)
                last.then_inc(msg_ready, 1)

            def mask_early(b, i):
                tr = tr1[EARLY[i] % TR1]
                if not is_start(b) or i >= EARLY1:
                    dve.wait_ge(early_stored[i % EARLY1], b * (NE // EARLY1 * 16) + i // EARLY1 * 16)
                dve.wait_ge(transposed, b * CHUNKS + (EARLY[i] + 1))
                nc.vector.scalar_tensor_tensor(early1[i % EARLY1][:], tr[:], 1.0, tr[:],
                                               ALU.is_lt, ALU.mult).then_inc(early_masked, 1)

            def layer1(b, e, parity, start, e_start):
                for c in range(CHUNKS):
                    dve.wait_ge(low_loaded[c % RAW1], (b * USES + (c // RAW1 + 1)) * (Q // 2 * 16))
                    dve.wait_ge(high_loaded[c % RAW1], (b * USES + (c // RAW1 + 1)) * (Q // 2 * 16))
                    if not start or c >= TR1:
                        dve.wait_ge(multiplied, b * CHUNKS + (c + 1 - TR1))
                    if c - TR1 in EARLY:
                        dve.wait_ge(early_masked, b * NE + (EARLY.index(c - TR1) + 1))
                    nc.vector.transpose(tr1[c % TR1][:], raw1[c % RAW1][:]).then_inc(transposed, 1)
                    if c - 1 in EARLY:
                        mask_early(b, EARLY.index(c - 1))
                    if e is not None:
                        if c == 2:
                            add_and_stats(e, 0, 1 - parity, e_start)
                        if c == 4:
                            normalise(e)
                        if c == 8:
                            msg_bias(e, e_start)

            layer1(0, None, 0, True, False)
            layer1(1, 0, 1, False, True)
            with dve.Fori(2, BLOCKS - 1, 2) as b:
                layer1(b, b - 1, 0, False, False)
                layer1(b + 1, b, 1, False, False)
            last_block = BLOCKS - 1
            layer1(last_block, last_block - 1, last_block % 2, False, False)

            def late_masks(b, parity, pair):
                for i in (2 * pair, 2 * pair + 1):
                    at = slot(parity, i, NL, RAW2)
                    done = (b - parity) * (NL * Q // 2 * 16 // RAW2) + ((parity * NL + i) // RAW2 + 1) * (Q // 2 * 16)
                    dve.wait_ge(late_low_loaded[at], done)
                    dve.wait_ge(late_high_loaded[at], done)
                    nc.vector.scalar_tensor_tensor(raw2[at][:], raw2[at][:], 1.0, raw2[at][:],
                                                   ALU.is_lt, ALU.mult).then_inc(masked, 1)

            def square_late(b, parity, pair):
                tr = tr2[slot(parity, 2 * pair, NL, TR2)]
                dve.wait_ge(inverted, b * NL + (BLOCKS * NE + 2 * pair + 1))
                nc.vector.scalar_tensor_tensor(tr[:], tr[:], 2.0, tr[:], ALU.subtract, ALU.mult).then_inc(dve_squared, 1)

            def late_transposes(b, parity, pair):
                for i in (2 * pair, 2 * pair + 1):
                    at = slot(parity, i, NL, TR2)
                    if is_start(b) and i < TR2:
                        wait_layer1(dve, tr2[at])
                    else:
                        dve.wait_ge(late_multiplied, b * NL + (i + 1 - TR2))
                    dve.wait_ge(masked, b * NL + (i + 1))
                    nc.vector.transpose(tr2[at][:], raw2[slot(parity, i, NL, RAW2)][:]).then_inc(late_transposed, 1)

            def first_pair(b, parity):
                late_masks(b, parity, 0)
                if not is_start(b):
                    square_late(b - 1, 1 - parity, PAIRS - 1)
                late_transposes(b, parity, 0)

            def layer2(b, e, parity):
                for pair in range(1, PAIRS):
                    late_masks(b, parity, pair)
                    square_late(b, parity, pair - 1)
                    late_transposes(b, parity, pair)
                    if e is None and pair == 1:
                        dve.wait_ge(msg_loaded, Q * 16)
                        clear_duplicates(msg_masked)
                if e is not None:
                    add_and_stats(e, 1, 1 - parity, False)
                    normalise(e + BLOCKS)

            first_pair(0, 0)
            add_and_stats(last_block, 0, last_block % 2, False)
            normalise(last_block)
            msg_bias(last_block, False)
            layer2(0, None, 0)
            with dve.Fori(1, BLOCKS - 1, 2) as b:
                first_pair(b, 1)
                layer2(b, b - 1, 1)
                first_pair(b + 1, 0)
                layer2(b + 1, b, 0)
            square_late(last_block, 0, PAIRS - 1)
            add_and_stats(last_block, 1, last_block % 2, False)
            normalise(last_block + BLOCKS)

        @block.tensor
        def _(pe):
            pe.wait_ge(consts_loaded, 6 * 16)
            pe.wait_ge(masks_ready, Q)
            nc.tensor.transpose(p_xt[:, 0:D], w_item_nat, ident[:])
            nc.tensor.transpose(p_xt[:, D:2 * D], w_user_nat, ident[:]).then_inc(w_transposed, 1)
            pe.wait_ge(w_copied, 2)
            pe.wait_ge(items_loaded, Q * 16)

            def item_transposes(k):
                if k >= 2:
                    pe.wait_ge(item_t_copied, k - 1)
                for j in range(SUB):
                    last = nc.tensor.transpose((p_xt, p_x1t)[k % 2][:, j * P:(j + 1) * P], feat[:, k * SUB + j, :], ident[:])
                last.then_inc(item_transposed, 1)

            item_transposes(0)
            for k in range(GROUPS):
                if k + 1 < GROUPS:
                    item_transposes(k + 1)
                pe.wait_ge(item_t_copied, k + 1)
                if k >= 2:
                    pe.wait_ge(item_features, k - 1)
                for j in range(SUB):
                    last = nc.tensor.matmul((p_z, p_msg)[k % 2][:, j, :], (x_t, x1_t)[k % 2][:, j * P:(j + 1) * P], w_item_t[:],
                                            start=True, stop=True)
                last.then_inc(item_product, 1)
            pe.wait_ge(features_ready, DUPS)

            def chunk_products(parity, c, buffer, first, last_of_block):
                moving = buffer[:].rearrange("p (r j s) -> p r j s", r=RG, j=CB)
                for j in range(CB):
                    last = nc.tensor.matmul(acc[parity][:], feat[:, c * CB + j, :], moving[:, :, j, :],
                                            start=(first and j == 0), stop=(last_of_block and j == CB - 1))
                return last

            def z_transposes(ge, start):
                pe.wait_ge(z_t_ready, ge + 1)
                if not start:
                    pe.wait_ge(res_added, ge)
                for s in range(SUB):
                    last = nc.tensor.transpose(p_z[0:SP_ROWS, s, :], z_t[:, s * SP_ROWS:(s + 1) * SP_ROWS], ident[:])
                last.then_inc(z_transposed, 1)

            def x_transposes(b, parity, start):
                pe.wait_ge(x_loaded[parity], (b - parity) * 8 + 16)
                if not start:
                    pe.wait_ge(x_t_ready, b)
                for s in range(SUB):
                    last = nc.tensor.transpose(p_xt[:, s * SP_ROWS:(s + 1) * SP_ROWS], x_rows[parity][:, s, :],
                                               ident[0:SP_ROWS, 0:SP_ROWS])
                last.then_inc(x_transposed, 1)

            def x1_transposes(e, start):
                pe.wait_ge(normed, e + 1)
                if not start:
                    pe.wait_ge(x1_t_ready, e)
                for s in range(SUB):
                    last = nc.tensor.transpose(p_x1t[:, s * SP_ROWS:(s + 1) * SP_ROWS], res[:, s, :],
                                               ident[0:SP_ROWS, 0:SP_ROWS])
                last.then_inc(x1_transposed, 1)

            def msg_products(e, start):
                pe.wait_ge(x1_t_ready, e + 1)
                if not start:
                    pe.wait_ge(msg_ready, e)
                for s in range(SUB):
                    last = nc.tensor.matmul(p_msg[0:SP_ROWS, s, :], x1_t[:, s * SP_ROWS:(s + 1) * SP_ROWS], w_msg_sb[:],
                                            start=True, stop=True)
                last.then_inc(msg_product, 1)

            def layer1(b, e, parity, e_start):
                if e is not None and not e_start:
                    pe.wait_ge(z_t_ready, b - 1)
                for c in range(CHUNKS):
                    pe.wait_ge(transposed, b * CHUNKS + (c + 1))
                    chunk_products(parity, c, tr1[c % TR1], c == 0, False).then_inc(multiplied, 1)
                    if c == 1:
                        x_transposes(b, parity, e is None)
                    if e is not None:
                        if c == 0:
                            z_transposes(e, e_start)
                        if c == 4:
                            x1_transposes(e, e_start)
                        if c == 6:
                            msg_products(e, e_start)
                pe.wait_ge(x_t_ready, b + 1)
                nc.tensor.matmul(acc[parity][:], w_user_t[:], x_t[:, 0:BLOCK], start=False, stop=True).then_inc(sums_done, 1)

            layer1(0, None, 0, False)
            layer1(1, 0, 1, True)
            layer1(2, 1, 0, False)
            with pe.Fori(3, BLOCKS - 1, 2) as b:
                layer1(b, b - 1, 1, False)
                layer1(b + 1, b, 0, False)
            last_block = BLOCKS - 1
            z_transposes(last_block, False)
            x1_transposes(last_block, False)
            msg_products(last_block, False)

            pe.wait_ge(msg_loaded, Q * 16)

            def late_products(b, parity, i):
                pe.wait_ge(weighted, b * NL + (BLOCKS * NE + i + 1))
                chunk_products((parity + BLOCKS) % 2, LATE[i], tr2[slot(parity, i, NL, TR2)], i == 0,
                               i == NL - 1).then_inc(late_multiplied, 1)

            def early_products(b, parity, i):
                pe.wait_ge(early_loaded[i % EARLY2], b * (NE // EARLY2 * 16) + (i // EARLY2 + 1) * 16)
                chunk_products((parity + BLOCKS) % 2, EARLY[i], early2[i % EARLY2], False,
                               False).then_inc(early_multiplied, 1)

            def layer2(b, e, parity):
                pe.wait_ge(z_t_ready, b + (BLOCKS - 1))
                for pair in range(PAIRS):
                    late_products(b, parity, 2 * pair)
                    last_ones = pair == PAIRS - 1
                    if last_ones:
                        for i in AFTER_PAIR[pair]:
                            early_products(b, parity, i)
                        if e is None:
                            pe.wait_ge(msg_masked, DUPS)
                    late_products(b, parity, 2 * pair + 1)
                    if not last_ones:
                        for i in AFTER_PAIR[pair]:
                            early_products(b, parity, i)
                    if e is not None and pair == 0:
                        z_transposes(e + BLOCKS, False)

            layer2(0, None, 0)
            with pe.Fori(1, BLOCKS - 1, 2) as b:
                layer2(b, b - 1, 1)
                layer2(b + 1, b, 0)
            z_transposes(last_block + BLOCKS, False)


_INS = ['x', 'adj', 'L0_gnn_item_feat', 'L0_gnn_W_item', 'L0_gnn_b_item', 'L0_gnn_W_user', 'L0_gnn_b_user',
        'L1_gnn_W', 'L1_gnn_B']
_OUTS = [((10000, 128), 'float32')]


def kernel(**inputs):
    import numpy as _np
    import concourse.bacc as _bacc
    from concourse import mybir as _mybir
    from concourse.bass_utils import run_bass_kernel_spmd as _run

    nc = _bacc.Bacc("TRN2", target_bir_lowering=False, num_devices=1)
    arrays, args = {}, []
    for name in _INS:
        a = _np.ascontiguousarray(inputs[name])
        arrays[f"in_{name}_dram"] = a
        args.append(nc.dram_tensor(f"in_{name}_dram", a.shape, _mybir.dt.from_np(a.dtype), kind="ExternalInput").ap())
    for i, (shape, dtype) in enumerate(_OUTS):
        dt = _mybir.dt.from_np(_np.dtype(dtype))
        args.append(nc.dram_tensor(f"out_{i}_dram", shape, dt, kind="ExternalOutput").ap())
    two_graph_layers(nc, *args)
    r = _run(nc, [arrays], core_ids=[0])
    return r.results[0]["out_0_dram"]
```

```python
import numpy as np
from contextlib import ExitStack

import concourse.bass as bass
from concourse import mybir


def two_graph_layers(nc, x, adj, item, w_item, b_item, w_user, b_user, w_msg, b_msg, out):
    F32 = mybir.dt.float32
    ALU = mybir.AluOpType
    ACT = mybir.ActivationFunctionType

    N, D = x.shape
    P = 128
    S = 32
    Q = P // S
    COLBLOCKS = -(-N // (Q * S))
    QCOLS = COLBLOCKS * S
    START = [q * (N - QCOLS) // (Q - 1) for q in range(Q)]
    FRESH = [START[q + 1] - START[q] for q in range(Q - 1)] + [QCOLS]
    CHUNKS = 10
    CB = -(-COLBLOCKS // CHUNKS)
    CCOLS = CB * S
    RG = 15
    BLOCK = RG * S
    BLOCKS = 21
    BSTRIDE = (N - BLOCK) // (BLOCKS - 1)
    assert BSTRIDE * (BLOCKS - 1) + BLOCK == N and BSTRIDE <= BLOCK
    SUB = 4
    SP_ROWS = BLOCK // SUB
    CHUNK = RG * CCOLS

    def col_blocks(c):
        return min(CB, COLBLOCKS - c * CB)

    def size(c):
        return RG * col_blocks(c) * S

    EARLY = [1, 3, 5, 7]
    LATE = [c for c in range(CHUNKS) if c not in EARLY]
    NE, NL = len(EARLY), len(LATE)
    DVE_SQUARES = [0, 2, 3, 4]
    ACT_SQUARES = [i for i in range(NL) if i not in DVE_SQUARES]
    assert NE < NL
    RAW1, TR1, EARLY1 = 5, 2, 2
    RAW2, EARLY2, TR2 = 4, 2, 4
    NBUF = max(RAW1 + TR1 + EARLY1, RAW2 + EARLY2 + TR2)
    EPS = 1e-5
    TINY = 2.0 ** -60
    FIRST_DUP = min(FRESH) // S
    DUPS = COLBLOCKS - FIRST_DUP
    DUP_LATE = LATE.index(FIRST_DUP // CB)
    assert FIRST_DUP // CB == CHUNKS - 1
    GROUPS = -(-COLBLOCKS // SUB)

    x1_dram = nc.dram_tensor("x1_scratch", (N, D), F32, kind="Internal").ap()
    early_dram = nc.dram_tensor("early_weights", (BLOCKS * NE * P, CHUNK), F32, kind="Internal").ap()
    msg_dram = nc.dram_tensor("msg_scratch", (N, D), F32, kind="Internal").ap()

    def block_rows(dram, b):
        return dram[bass.ds(b * BSTRIDE, BLOCK), :].rearrange("(q p) d -> p q d", p=SP_ROWS)

    def stretch(dram, q):
        return dram[START[q]:START[q] + QCOLS, :].rearrange("(j p) d -> p j d", p=S)

    HALF = CHUNKS // 2 * CB
    assert HALF % SUB == 0

    def group(k):
        return range(k * SUB, min((k + 1) * SUB, COLBLOCKS))

    def load_features(eng, dram, half, loaded):
        cols = slice(0, HALF) if half == 0 else slice(HALF, COLBLOCKS)
        for q in range(Q):
            eng.dma_start(feat[q * S:(q + 1) * S, cols, :], stretch(dram, q)[:, cols, :]).then_inc(loaded[half], 16)

    def chunk_cols(c, q):
        return min(col_blocks(c) * S, FRESH[q] - c * CCOLS)

    def adj_chunk(b, c, q):
        rows = adj[bass.ds(b * BSTRIDE, BLOCK), :].rearrange("(r p) n -> p r n", p=S)
        first = START[q] + c * CCOLS
        return rows[:, :, first:first + chunk_cols(c, q)]

    def slot(parity, i, per_block, ring):
        assert 2 * per_block % ring == 0
        return (parity * per_block + i) % ring

    def early_weights(b, i):
        return early_dram[bass.ds(b * (NE * P) + i * P, P), :]

    ctx = ExitStack()
    with ctx:
        def sb(name, shape):
            return ctx.enter_context(nc.sbuf_tensor(name, shape, F32))

        def ps(name, shape):
            return ctx.enter_context(nc.psum_tensor(name, shape, F32))

        def sem(name):
            return ctx.enter_context(nc.semaphore(name))

        feat = sb("feat", [P, COLBLOCKS, D])
        chunks = [sb(f"chunk{i}", [P, CHUNK]) for i in range(NBUF)]
        raw1, tr1, early1 = chunks[0:RAW1], chunks[RAW1:RAW1 + TR1], chunks[RAW1 + TR1:RAW1 + TR1 + EARLY1]
        raw2, early2, tr2 = chunks[0:RAW2], chunks[RAW2:RAW2 + EARLY2], chunks[RAW2 + EARLY2:RAW2 + EARLY2 + TR2]
        ident = sb("ident", [P, P])
        first_named = sb("first_named", [P, COLBLOCKS])
        w_item_t = sb("w_item_t", [D, D])
        w_user_t = sb("w_user_t", [D, D])
        w_msg_sb = sb("w_msg_sb", [D, D])
        b_item_bc = sb("b_item_bc", [P, D])
        b_msg_bc = sb("b_msg_bc", [P, D])
        b_user_col = sb("b_user_col", [D, 1])
        x_rows = [sb(f"x_rows{i}", [SP_ROWS, SUB, D]) for i in range(2)]
        x_t = sb("x_t", [D, SUB * P])
        z_t = sb("z_t", [D, BLOCK])
        w_item_nat, w_user_nat = z_t[:, 0:D], z_t[:, D:2 * D]
        res = sb("res", [SP_ROWS, SUB, D])
        x1_t = sb("x1_t", [D, SUB * P])
        msg = sb("msg", [SP_ROWS, SUB, D])
        stats = sb("stats", [SP_ROWS, SUB, 6])
        meanvar = sb("meanvar", [SP_ROWS, SUB, 2])
        var_eps = sb("var_eps", [SP_ROWS, SUB])
        log_var = sb("log_var", [SP_ROWS, SUB])
        rstd0 = sb("rstd0", [SP_ROWS, SUB])
        newton = sb("newton", [SP_ROWS, SUB])
        rstd = sb("rstd", [SP_ROWS, SUB])

        acc = [ps(f"acc{i}", [D, BLOCK]) for i in range(2)]
        p_xt = ps("p_xt", [D, SUB * P])
        p_z = ps("p_z", [P, SUB, D])
        p_x1t = ps("p_x1t", [D, SUB * P])
        p_msg = ps("p_msg", [P, SUB, D])

        consts_loaded = sem("consts_loaded")
        items_loaded = [sem(f"items_loaded{i}") for i in range(2)]
        ident_zeroed = sem("ident_zeroed")
        masks_set = sem("masks_set")
        masks_ready = sem("masks_ready")
        w_transposed = sem("w_transposed")
        w_copied = sem("w_copied")
        item_transposed = sem("item_transposed")
        item_t_copied = sem("item_t_copied")
        item_product = sem("item_product")
        item_features = sem("item_features")
        features_ready = sem("features_ready")
        low_loaded = [sem(f"low_loaded{i}") for i in range(RAW1)]
        high_loaded = [sem(f"high_loaded{i}") for i in range(RAW1)]
        late_low_loaded = [sem(f"late_low_loaded{i}") for i in range(RAW2)]
        late_high_loaded = [sem(f"late_high_loaded{i}") for i in range(RAW2)]
        transposed = sem("transposed")
        multiplied = sem("multiplied")
        early_masked = sem("early_masked")
        early_stored = [sem(f"early_stored{i}") for i in range(EARLY1)]
        masked = sem("masked")
        late_transposed = sem("late_transposed")
        late_multiplied = sem("late_multiplied")
        early_loaded = [sem(f"early_loaded{i}") for i in range(EARLY2)]
        early_multiplied = sem("early_multiplied")
        logged = sem("logged")
        inverted = sem("inverted")
        squared = sem("squared")
        dve_squared = sem("dve_squared")
        weighted = sem("weighted")
        x_loaded = [sem(f"x_loaded{i}") for i in range(2)]
        x_transposed = sem("x_transposed")
        x_t_ready = sem("x_t_ready")
        sums_done = sem("sums_done")
        z_t_ready = sem("z_t_ready")
        z_transposed = sem("z_transposed")
        res_loaded = sem("res_loaded")
        res_added = sem("res_added")
        norm_step = sem("norm_step")
        var_ready = sem("var_ready")
        log_var_ready = sem("log_var_ready")
        rstd0_ready = sem("rstd0_ready")
        rstd_refined = sem("rstd_refined")
        normed = sem("normed")
        x1_transposed = sem("x1_transposed")
        x1_t_ready = sem("x1_t_ready")
        msg_product = sem("msg_product")
        msg_ready = sem("msg_ready")
        x1_stored = sem("x1_stored")
        msg_stored = sem("msg_stored")
        msg_loaded = [sem(f"msg_loaded{i}") for i in range(2)]
        msg_masked = sem("msg_masked")
        out_stored = sem("out_stored")

        block = ctx.enter_context(nc.Block())

        def is_start(b):
            return isinstance(b, int) and b == 0

        def last_use(ring, at, of_all):
            return of_all - (of_all - 1 - at) % ring

        def wait_layer1(eng, buffer):
            n = chunks.index(buffer)
            if n < RAW1:
                eng.wait_ge(transposed, last_use(RAW1, n, BLOCKS * CHUNKS))
            elif n < RAW1 + TR1:
                eng.wait_ge(multiplied, last_use(TR1, n - RAW1, BLOCKS * CHUNKS))
            elif n < RAW1 + TR1 + EARLY1:
                eng.wait_ge(early_stored[n - RAW1 - TR1], BLOCKS * NE // EARLY1 * 16)

        def load_early(eng, b, i):
            at = i % EARLY2
            if is_start(b) and i < EARLY2:
                wait_layer1(eng, early2[at])
            else:
                eng.wait_ge(early_multiplied, b * NE + (i + 1 - EARLY2))
            eng.dma_start(early2[at][:], early_weights(b, i)).then_inc(early_loaded[at], 16)

        def load_adj(eng, buffer, b, c, quadrants, loaded):
            view = buffer[:, 0:size(c)].rearrange("p (r n) -> p r n", r=RG)
            for q in quadrants:
                eng.dma_start(view[q * S:(q + 1) * S, :, 0:chunk_cols(c, q)], adj_chunk(b, c, q)).then_inc(loaded, 16)

        def load_raw(eng, b, parity, quadrants, loaded, which):
            for c in which:
                if not is_start(b) or c >= RAW1:
                    eng.wait_ge(transposed, b * CHUNKS + (c + 1 - RAW1))
                at = slot(parity, c, CHUNKS, RAW1)
                load_adj(eng, raw1[at], b, c, quadrants, loaded[at])

        def load_late(eng, b, parity, quadrants, loaded, which):
            for i in which:
                at = slot(parity, i, NL, RAW2)
                if is_start(b) and i < RAW2:
                    wait_layer1(eng, raw2[at])
                else:
                    eng.wait_ge(late_transposed, b * NL + (i + 1 - RAW2))
                load_adj(eng, raw2[at], b, LATE[i], quadrants, loaded[at])

        @block.sync
        def _(sp):
            def load_x(b, parity, first_two=False):
                if not first_two:
                    sp.wait_ge(res_added, b - 1)
                sp.dma_start(x_rows[parity][:], block_rows(x, b)).then_inc(x_loaded[parity], 16)

            def layer1(b, parity, first_two=False):
                load_x(b, parity, first_two)
                load_raw(sp, b, parity, (0, 1), low_loaded, range(CHUNKS))

            def load_messages(half):
                load_features(sp, msg_dram, half, msg_loaded)

            load_features(sp, item, 0, items_loaded)
            load_raw(sp, 0, 0, (0, 1), low_loaded, [0])
            load_features(sp, item, 1, items_loaded)
            load_x(0, 0, True)
            load_raw(sp, 0, 0, (0, 1), low_loaded, range(1, CHUNKS))
            layer1(1, 1, True)
            layer1(2, 0)
            with sp.Fori(3, BLOCKS - 1, 2) as b:
                layer1(b, 1)
                layer1(b + 1, 0)
            load_late(sp, 0, 0, (0, 1), late_low_loaded, range(RAW2))

            last = BLOCKS - 1
            sp.wait_ge(msg_ready, BLOCKS)
            sp.wait_ge(msg_stored, last * 16)
            sp.dma_start(block_rows(msg_dram, last), msg[:]).then_inc(msg_stored, 16)
            sp.wait_ge(msg_stored, BLOCKS * 16)
            sp.wait_ge(sums_done, BLOCKS)
            load_messages(0)
            for i in range(EARLY1):
                sp.wait_ge(early_stored[i], BLOCKS * NE // EARLY1 * 16)
            load_early(sp, 0, 0)
            load_late(sp, 0, 0, (0, 1), late_low_loaded, [RAW2])
            load_early(sp, 0, 1)
            load_late(sp, 0, 0, (0, 1), late_low_loaded, range(RAW2 + 1, NL))
            load_messages(1)

            with sp.Fori(1, BLOCKS - 1, 2) as b:
                load_late(sp, b, 1, (0, 1), late_low_loaded, range(NL))
                load_late(sp, b + 1, 0, (0, 1), late_low_loaded, range(NL))

        @block.gpsimd
        def _(pool):
            nc.gpsimd.memset(ident[:], 0.0).then_inc(ident_zeroed, 1)
            nc.gpsimd.memset(first_named[:], 1.0).then_inc(masks_set, 1)
            pool.wait_ge(ident_zeroed, 1)
            nc.gpsimd.affine_select(out=ident[:], in_=ident[:], compare_op=ALU.not_equal, fill=1.0, base=0,
                                    pattern=[[-1, P]], channel_multiplier=1).then_inc(masks_ready, 1)
            pool.wait_ge(masks_set, 1)
            for q in range(Q - 1):
                pool.wait_ge(masks_ready, q + 1)
                part = first_named[q * S:(q + 1) * S, :]
                nc.gpsimd.affine_select(out=part, in_=part, compare_op=ALU.is_ge, fill=0.0, base=FRESH[q] - 1,
                                        pattern=[[-S, COLBLOCKS]], channel_multiplier=-1).then_inc(masks_ready, 1)
            load_raw(pool, 0, 0, (2, 3), high_loaded, range(CHUNKS))
            with pool.Fori(1, BLOCKS - 1, 2) as b:
                load_raw(pool, b, 1, (2, 3), high_loaded, range(CHUNKS))
                load_raw(pool, b + 1, 0, (2, 3), high_loaded, range(CHUNKS))
            load_late(pool, 0, 0, (2, 3), late_high_loaded, range(RAW2))
            pool.wait_ge(msg_loaded[0], Q * 16)
            load_late(pool, 0, 0, (2, 3), late_high_loaded, range(RAW2, NL))
            with pool.Fori(1, BLOCKS - 1, 2) as b:
                load_late(pool, b, 1, (2, 3), late_high_loaded, range(NL))
                load_late(pool, b + 1, 0, (2, 3), late_high_loaded, range(NL))

        @block.scalar
        def _(act):
            nc.scalar.preload_act_table_set("natural_log_exp_and_others")
            act.dma_start(w_item_nat, w_item).then_inc(consts_loaded, 16)
            act.dma_start(w_user_nat, w_user).then_inc(consts_loaded, 16)
            act.dma_start(w_msg_sb[:], w_msg).then_inc(consts_loaded, 16)
            act.dma_start(b_item_bc[:], b_item.rearrange("(a d) -> a d", a=1).to_broadcast([P, D])).then_inc(consts_loaded, 16)
            act.dma_start(b_msg_bc[:], b_msg.rearrange("(a d) -> a d", a=1).to_broadcast([P, D])).then_inc(consts_loaded, 16)
            act.dma_start(b_user_col[:], b_user.rearrange("(d a) -> d a", a=1)).then_inc(consts_loaded, 16)
            act.wait_ge(w_transposed, 1)
            nc.scalar.activation(w_item_t[:], p_xt[:, 0:D], ACT.Copy).then_inc(w_copied, 1)
            nc.scalar.activation(w_user_t[:], p_xt[:, D:2 * D], ACT.Copy).then_inc(w_copied, 1)
            for k in range(GROUPS):
                act.wait_ge(item_transposed, k + 1)
                if k >= 2:
                    act.wait_ge(item_product, k - 1)
                cols = len(group(k)) * P
                nc.scalar.activation((x_t, x1_t)[k % 2][:, 0:cols], (p_xt, p_x1t)[k % 2][:, 0:cols], ACT.Copy).then_inc(item_t_copied, 1)
            act.wait_ge(item_product, GROUPS)
            act.wait_ge(consts_loaded, 6 * 16)

            def sums_out(e, layer, parity):
                ge = e + layer * BLOCKS
                if layer:
                    act.wait_ge(x1_stored, BLOCKS * 16)
                    if not is_start(e):
                        act.wait_ge(out_stored, e * 16)
                    act.dma_start(res[:], block_rows(x1_dram, e)).then_inc(res_loaded, 16)
                    act.wait_ge(late_multiplied, e * NL + NL)
                else:
                    act.wait_ge(sums_done, ge + 1)
                if layer or not is_start(e):
                    act.wait_ge(z_transposed, ge)
                if layer:
                    nc.scalar.activation(z_t[:], acc[(parity + BLOCKS) % 2][:], ACT.Copy).then_inc(z_t_ready, 1)
                else:
                    nc.scalar.activation(z_t[:], acc[parity][:], ACT.Relu, bias=b_user_col[:]).then_inc(z_t_ready, 1)

            def rstd_guess(ge):
                act.wait_ge(var_ready, ge + 1)
                nc.scalar.activation(log_var[:], var_eps[:], ACT.Ln).then_inc(log_var_ready, 1)
                act.wait_ge(log_var_ready, ge + 1)
                nc.scalar.activation(rstd0[:], log_var[:], ACT.Exp, scale=-0.5).then_inc(rstd0_ready, 1)

            def x_t_out(b):
                act.wait_ge(x_transposed, b + 1)
                if not is_start(b):
                    act.wait_ge(sums_done, b)
                nc.scalar.activation(x_t[:, 0:BLOCK], p_xt[:, 0:BLOCK], ACT.Copy).then_inc(x_t_ready, 1)

            def x1_out(e):
                act.wait_ge(x1_transposed, e + 1)
                if not is_start(e):
                    act.wait_ge(msg_product, e)
                nc.scalar.activation(x1_t[:, 0:BLOCK], p_x1t[:, 0:BLOCK], ACT.Copy).then_inc(x1_t_ready, 1)
                act.wait_ge(normed, e + 1)
                act.dma_start(block_rows(x1_dram, e), res[:]).then_inc(x1_stored, 16)

            def msg_out(e):
                act.wait_ge(msg_ready, e + 1)
                if not is_start(e):
                    act.wait_ge(msg_stored, e * 16)
                act.dma_start(block_rows(msg_dram, e), msg[:]).then_inc(msg_stored, 16)

            def log(buffer):
                nc.scalar.activation(buffer, buffer, ACT.Ln, bias=TINY).then_inc(logged, 1)

            def invert(buffer, nth):
                act.wait_ge(logged, nth)
                nc.scalar.activation(buffer, buffer, ACT.Exp, scale=-1.0).then_inc(inverted, 1)

            def square(buffer, nth):
                act.wait_ge(inverted, nth)
                nc.scalar.activation(buffer, buffer, ACT.Square, bias=-1.0).then_inc(squared, 1)

            def weigh(buffer, nth):
                act.wait_ge(squared, nth)
                nc.scalar.activation(buffer, buffer, ACT.Exp, scale=-2.0).then_inc(weighted, 1)

            def early_chunk(b, i):
                buffer = early1[i % EARLY1][:]
                nth = b * NE + (i + 1)
                act.wait_ge(early_masked, nth)
                log(buffer)
                invert(buffer, nth)
                square(buffer, nth)
                weigh(buffer, nth)
                act.wait_ge(weighted, nth)
                act.dma_start(early_weights(b, i), buffer).then_inc(early_stored[i % EARLY1], 16)

            def layer1(b, e, parity):
                if e is not None:
                    sums_out(e, 0, 1 - parity)
                x_t_out(b)
                if e is not None:
                    rstd_guess(e)
                early_chunk(b, 0)
                early_chunk(b, 1)
                if e is not None:
                    x1_out(e)
                early_chunk(b, 2)
                early_chunk(b, 3)
                if e is not None:
                    msg_out(e)

            layer1(0, None, 0)
            layer1(1, 0, 1)
            layer1(2, 1, 0)
            with act.Fori(3, BLOCKS - 1, 2) as b:
                layer1(b, b - 1, 1)
                layer1(b + 1, b, 0)
            last = BLOCKS - 1

            def store_out(e):
                act.wait_ge(normed, e + (BLOCKS + 1))
                act.dma_start(block_rows(out, e), res[:]).then_inc(out_stored, 16)

            def end_of_layer1():
                sums_out(last, 0, last % 2)
                act.wait_ge(late_transposed, 1)
                log(tr2[0][:])
                rstd_guess(last)
                invert(tr2[0][:], BLOCKS * NE + 1)
                x1_out(last)
                act.wait_ge(dve_squared, 1)
                nc.scalar.activation(tr2[0][:], tr2[0][:], ACT.Exp, bias=-2.0, scale=-2.0).then_inc(weighted, 1)

            def layer2(b, e, parity):
                k = b * NL
                nth = k + BLOCKS * NE
                tr = [tr2[slot(parity, i, NL, TR2)][:, 0:size(LATE[i])] for i in range(NL)]

                def log_late(i):
                    act.wait_ge(late_transposed, k + (i + 1))
                    log(tr[i])

                def invert_late(i):
                    invert(tr[i], nth + (i + 1))

                def square_late(i):
                    act.wait_ge(inverted, nth + (i + 1))
                    nc.scalar.activation(tr[i], tr[i], ACT.Square, bias=-1.0).then_inc(squared, 1)

                def weigh_late(i):
                    if i in DVE_SQUARES:
                        act.wait_ge(dve_squared, b * len(DVE_SQUARES) + (DVE_SQUARES.index(i) + 1))
                        nc.scalar.activation(tr[i], tr[i], ACT.Exp, bias=-2.0, scale=-2.0).then_inc(weighted, 1)
                    else:
                        weigh(tr[i], b * len(ACT_SQUARES) + (BLOCKS * NE + ACT_SQUARES.index(i) + 1))

                if is_start(b):
                    end_of_layer1()
                else:
                    log_late(0)
                    invert_late(0)
                log_late(1)
                if not is_start(b):
                    load_early(act, b, 0)
                invert_late(1)
                if not is_start(b):
                    weigh_late(0)
                square_late(1)
                log_late(2)
                if not is_start(b):
                    load_early(act, b, 1)
                invert_late(2)
                weigh_late(1)
                if e is not None:
                    sums_out(e, 1, 1 - parity)
                log_late(3)
                weigh_late(2)
                invert_late(3)
                load_early(act, b, 2)
                log_late(4)
                if e is not None:
                    rstd_guess(e + BLOCKS)
                invert_late(4)
                weigh_late(3)
                load_early(act, b, 3)
                log_late(5)
                invert_late(5)
                square_late(5)
                if e is not None:
                    store_out(e)
                weigh_late(4)
                weigh_late(5)

            layer2(0, None, 0)
            layer2(1, 0, 1)
            layer2(2, 1, 0)
            with act.Fori(3, BLOCKS - 1, 2) as b:
                layer2(b, b - 1, 1)
                layer2(b + 1, b, 0)
            sums_out(last, 1, last % 2)
            rstd_guess(last + BLOCKS)
            store_out(last)
            act.wait_ge(out_stored, BLOCKS * 16)

        @block.vector
        def _(dve):
            USES = CHUNKS // RAW1
            assert CHUNKS % RAW1 == 0 and CHUNKS % TR1 == 0 and NE % EARLY1 == 0 and NE % EARLY2 == 0
            def transpose_chunk(b, c, start):
                dve.wait_ge(low_loaded[c % RAW1], (b * USES + (c // RAW1 + 1)) * (Q // 2 * 16))
                dve.wait_ge(high_loaded[c % RAW1], (b * USES + (c // RAW1 + 1)) * (Q // 2 * 16))
                if not start or c >= TR1:
                    dve.wait_ge(multiplied, b * CHUNKS + (c + 1 - TR1))
                if c - TR1 in EARLY:
                    dve.wait_ge(early_masked, b * NE + (EARLY.index(c - TR1) + 1))
                nc.vector.transpose(tr1[c % TR1][:, 0:size(c)], raw1[c % RAW1][:, 0:size(c)]).then_inc(transposed, 1)

            dve.wait_ge(consts_loaded, 6 * 16)
            transpose_chunk(0, 0, True)
            for k in range(GROUPS):
                dve.wait_ge(item_product, k + 1)
                for j, cb in enumerate(group(k)):
                    last = nc.vector.tensor_tensor(feat[:, cb, :], (p_z, p_msg)[k % 2][:, j, :], b_item_bc[:], ALU.add)
                last.then_inc(item_features, 1)
            dve.wait_ge(masks_ready, Q)
            dve.wait_ge(item_features, GROUPS)

            def clear_duplicates(signal):
                for j in range(FIRST_DUP, COLBLOCKS):
                    nc.vector.tensor_scalar(feat[:, j, :], feat[:, j, :], first_named[:, j:j + 1], None, ALU.mult).then_inc(signal, 1)

            clear_duplicates(features_ready)

            STEPS = 5

            def add_and_stats(e, layer, parity, start):
                ge = e + layer * BLOCKS
                if layer:
                    dve.wait_ge(res_loaded, e * 16 + 16)
                elif not start:
                    dve.wait_ge(x1_stored, e * 16)
                dve.wait_ge(z_transposed, ge + 1)
                nc.vector.tensor_tensor(res[:], res[:] if layer else x_rows[parity][:], p_z[0:SP_ROWS, :, :],
                                        ALU.add).then_inc(res_added, 1)
                dve.wait_ge(res_added, ge + 1)
                for s in range(SUB):
                    last = nc.vector.bn_stats(stats[:, s, :], res[:, s, :])
                last.then_inc(norm_step, 1)
                dve.wait_ge(norm_step, ge * STEPS + 1)
                nc.vector.memset(var_eps[:], EPS)
                for s in range(SUB):
                    last = nc.vector.bn_aggr(meanvar[:, s, :], stats[:, s, :])
                last.then_inc(norm_step, 1)
                dve.wait_ge(norm_step, ge * STEPS + 2)
                nc.vector.tensor_tensor(var_eps[:], var_eps[:], meanvar[:, :, 1], ALU.add).then_inc(var_ready, 1)

            def normalise(ge):
                dve.wait_ge(rstd0_ready, ge + 1)
                nc.vector.tensor_tensor(newton[:], rstd0[:], rstd0[:], ALU.mult).then_inc(norm_step, 1)
                dve.wait_ge(norm_step, ge * STEPS + 3)
                nc.vector.tensor_tensor(newton[:], newton[:], var_eps[:], ALU.mult).then_inc(norm_step, 1)
                dve.wait_ge(norm_step, ge * STEPS + 4)
                nc.vector.tensor_scalar(newton[:], newton[:], -0.5, 1.5, ALU.mult, ALU.add).then_inc(norm_step, 1)
                dve.wait_ge(norm_step, ge * STEPS + 5)
                nc.vector.tensor_tensor(rstd[:], newton[:], rstd0[:], ALU.mult).then_inc(rstd_refined, 1)
                dve.wait_ge(rstd_refined, ge + 1)
                for s in range(SUB):
                    last = nc.vector.tensor_scalar(res[:, s, :], res[:, s, :], meanvar[:, s, 0:1], rstd[:, s:s + 1],
                                                   ALU.subtract, ALU.mult)
                last.then_inc(normed, 1)

            def msg_bias(e, start):
                dve.wait_ge(msg_product, e + 1)
                if not start:
                    dve.wait_ge(msg_stored, e * 16)
                for s in range(SUB):
                    last = nc.vector.tensor_tensor(msg[:, s, :], p_msg[0:SP_ROWS, s, :], b_msg_bc[0:SP_ROWS, :], ALU.add)
                last.then_inc(msg_ready, 1)

            def mask_early(b, i):
                tr = tr1[EARLY[i] % TR1]
                if not is_start(b) or i >= EARLY1:
                    dve.wait_ge(early_stored[i % EARLY1], b * (NE // EARLY1 * 16) + i // EARLY1 * 16)
                dve.wait_ge(transposed, b * CHUNKS + (EARLY[i] + 1))
                nc.vector.scalar_tensor_tensor(early1[i % EARLY1][:], tr[:], 1.0, tr[:],
                                               ALU.is_lt, ALU.mult).then_inc(early_masked, 1)

            def layer1(b, e, parity, start, e_start):
                for c in range(CHUNKS):
                    if not start or c > 0:
                        transpose_chunk(b, c, start)
                    if c - 1 in EARLY:
                        mask_early(b, EARLY.index(c - 1))
                    if e is not None:
                        if c == 2:
                            add_and_stats(e, 0, 1 - parity, e_start)
                        if c == 4:
                            normalise(e)
                        if c == 8:
                            msg_bias(e, e_start)

            layer1(0, None, 0, True, False)
            layer1(1, 0, 1, False, True)
            with dve.Fori(2, BLOCKS - 1, 2) as b:
                layer1(b, b - 1, 0, False, False)
                layer1(b + 1, b, 1, False, False)
            last_block = BLOCKS - 1
            layer1(last_block, last_block - 1, last_block % 2, False, False)

            def mask_late(b, parity, i):
                at = slot(parity, i, NL, RAW2)
                done = (b - parity) * (NL * Q // 2 * 16 // RAW2) + ((parity * NL + i) // RAW2 + 1) * (Q // 2 * 16)
                dve.wait_ge(late_low_loaded[at], done)
                dve.wait_ge(late_high_loaded[at], done)
                raw = raw2[at][:, 0:size(LATE[i])]
                nc.vector.scalar_tensor_tensor(raw, raw, 1.0, raw,
                                               ALU.is_lt, ALU.mult).then_inc(masked, 1)

            def square_late(b, parity, i):
                tr = tr2[slot(parity, i, NL, TR2)][:, 0:size(LATE[i])]
                dve.wait_ge(inverted, b * NL + (BLOCKS * NE + i + 1))
                nc.vector.scalar_tensor_tensor(tr, tr, 2.0, tr, ALU.subtract, ALU.mult).then_inc(dve_squared, 1)

            def transpose_late(b, parity, i):
                at = slot(parity, i, NL, TR2)
                if is_start(b) and i < TR2:
                    wait_layer1(dve, tr2[at])
                else:
                    dve.wait_ge(late_multiplied, b * NL + (i + 1 - TR2))
                dve.wait_ge(masked, b * NL + (i + 1))
                nc.vector.transpose(tr2[at][:, 0:size(LATE[i])],
                                    raw2[slot(parity, i, NL, RAW2)][:, 0:size(LATE[i])]).then_inc(late_transposed, 1)

            def first_chunk(b, parity):
                mask_late(b, parity, 0)
                if not is_start(b):
                    square_late(b - 1, 1 - parity, 4)
                transpose_late(b, parity, 0)

            def layer2(b, e, parity):
                mask_late(b, parity, 1)
                transpose_late(b, parity, 1)
                mask_late(b, parity, 2)
                if not is_start(b):
                    square_late(b, parity, 0)
                transpose_late(b, parity, 2)
                mask_late(b, parity, 3)
                transpose_late(b, parity, 3)
                mask_late(b, parity, 4)
                square_late(b, parity, 2)
                transpose_late(b, parity, 4)
                mask_late(b, parity, 5)
                if e is not None:
                    add_and_stats(e, 1, 1 - parity, False)
                square_late(b, parity, 3)
                transpose_late(b, parity, 5)
                if e is None:
                    dve.wait_ge(msg_loaded[1], Q * 16)
                    clear_duplicates(msg_masked)
                if e is not None:
                    normalise(e + BLOCKS)

            first_chunk(0, 0)
            add_and_stats(last_block, 0, last_block % 2, False)
            normalise(last_block)
            msg_bias(last_block, False)
            square_late(0, 0, 0)
            layer2(0, None, 0)
            with dve.Fori(1, BLOCKS - 1, 2) as b:
                first_chunk(b, 1)
                layer2(b, b - 1, 1)
                first_chunk(b + 1, 0)
                layer2(b + 1, b, 0)
            square_late(last_block, 0, 4)
            add_and_stats(last_block, 1, last_block % 2, False)
            normalise(last_block + BLOCKS)

        @block.tensor
        def _(pe):
            pe.wait_ge(consts_loaded, 6 * 16)
            pe.wait_ge(masks_ready, Q)
            nc.tensor.transpose(p_xt[:, 0:D], w_item_nat, ident[:])
            nc.tensor.transpose(p_xt[:, D:2 * D], w_user_nat, ident[:]).then_inc(w_transposed, 1)
            pe.wait_ge(w_copied, 2)
            pe.wait_ge(items_loaded[0], Q * 16)

            def item_transposes(k):
                if k == HALF // SUB:
                    pe.wait_ge(items_loaded[1], Q * 16)
                if k >= 2:
                    pe.wait_ge(item_t_copied, k - 1)
                for j, cb in enumerate(group(k)):
                    last = nc.tensor.transpose((p_xt, p_x1t)[k % 2][:, j * P:(j + 1) * P], feat[:, cb, :], ident[:])
                last.then_inc(item_transposed, 1)

            item_transposes(0)
            for k in range(GROUPS):
                if k + 1 < GROUPS:
                    item_transposes(k + 1)
                pe.wait_ge(item_t_copied, k + 1)
                if k >= 2:
                    pe.wait_ge(item_features, k - 1)
                for j in range(len(group(k))):
                    last = nc.tensor.matmul((p_z, p_msg)[k % 2][:, j, :], (x_t, x1_t)[k % 2][:, j * P:(j + 1) * P], w_item_t[:],
                                            start=True, stop=True)
                last.then_inc(item_product, 1)
            pe.wait_ge(features_ready, DUPS)

            def chunk_products(parity, c, buffer, first, last_of_block):
                moving = buffer[:, 0:size(c)].rearrange("p (r j s) -> p r j s", r=RG, j=col_blocks(c))
                for j in range(col_blocks(c)):
                    last = nc.tensor.matmul(acc[parity][:], feat[:, c * CB + j, :], moving[:, :, j, :],
                                            start=(first and j == 0), stop=(last_of_block and j == col_blocks(c) - 1))
                return last

            def z_transposes(ge, start):
                pe.wait_ge(z_t_ready, ge + 1)
                if not start:
                    pe.wait_ge(res_added, ge)
                for s in range(SUB):
                    last = nc.tensor.transpose(p_z[0:SP_ROWS, s, :], z_t[:, s * SP_ROWS:(s + 1) * SP_ROWS], ident[:])
                last.then_inc(z_transposed, 1)

            def x_transposes(b, parity, start):
                pe.wait_ge(x_loaded[parity], (b - parity) * 8 + 16)
                if not start:
                    pe.wait_ge(x_t_ready, b)
                for s in range(SUB):
                    last = nc.tensor.transpose(p_xt[:, s * SP_ROWS:(s + 1) * SP_ROWS], x_rows[parity][:, s, :],
                                               ident[0:SP_ROWS, 0:SP_ROWS])
                last.then_inc(x_transposed, 1)

            def x1_transposes(e, start):
                pe.wait_ge(normed, e + 1)
                if not start:
                    pe.wait_ge(x1_t_ready, e)
                for s in range(SUB):
                    last = nc.tensor.transpose(p_x1t[:, s * SP_ROWS:(s + 1) * SP_ROWS], res[:, s, :],
                                               ident[0:SP_ROWS, 0:SP_ROWS])
                last.then_inc(x1_transposed, 1)

            def msg_products(e, start):
                pe.wait_ge(x1_t_ready, e + 1)
                if not start:
                    pe.wait_ge(msg_ready, e)
                for s in range(SUB):
                    last = nc.tensor.matmul(p_msg[0:SP_ROWS, s, :], x1_t[:, s * SP_ROWS:(s + 1) * SP_ROWS], w_msg_sb[:],
                                            start=True, stop=True)
                last.then_inc(msg_product, 1)

            def layer1(b, e, parity, e_start):
                if e is not None and not e_start:
                    pe.wait_ge(z_t_ready, b - 1)
                for c in range(CHUNKS):
                    pe.wait_ge(transposed, b * CHUNKS + (c + 1))
                    chunk_products(parity, c, tr1[c % TR1], c == 0, False).then_inc(multiplied, 1)
                    if c == 1:
                        x_transposes(b, parity, e is None)
                    if e is not None:
                        if c == 0:
                            z_transposes(e, e_start)
                        if c == 4:
                            x1_transposes(e, e_start)
                        if c == 6:
                            msg_products(e, e_start)
                pe.wait_ge(x_t_ready, b + 1)
                nc.tensor.matmul(acc[parity][:], w_user_t[:], x_t[:, 0:BLOCK], start=False, stop=True).then_inc(sums_done, 1)

            layer1(0, None, 0, False)
            layer1(1, 0, 1, True)
            layer1(2, 1, 0, False)
            with pe.Fori(3, BLOCKS - 1, 2) as b:
                layer1(b, b - 1, 1, False)
                layer1(b + 1, b, 0, False)
            last_block = BLOCKS - 1
            z_transposes(last_block, False)
            x1_transposes(last_block, False)
            msg_products(last_block, False)

            pe.wait_ge(msg_loaded[0], Q * 16)

            def second_half(c):
                if c * CB >= HALF:
                    pe.wait_ge(msg_loaded[1], Q * 16)

            def late_products(b, parity, i):
                if is_start(b):
                    second_half(LATE[i])
                pe.wait_ge(weighted, b * NL + (BLOCKS * NE + i + 1))
                chunk_products((parity + BLOCKS) % 2, LATE[i], tr2[slot(parity, i, NL, TR2)], i == 0,
                               i == NL - 1).then_inc(late_multiplied, 1)

            def early_products(b, parity, i):
                if is_start(b):
                    second_half(EARLY[i])
                pe.wait_ge(early_loaded[i % EARLY2], b * (NE // EARLY2 * 16) + (i // EARLY2 + 1) * 16)
                chunk_products((parity + BLOCKS) % 2, EARLY[i], early2[i % EARLY2], False,
                               False).then_inc(early_multiplied, 1)

            def layer2(b, e, parity):
                pe.wait_ge(z_t_ready, b + (BLOCKS - 1))
                for i in range(NL):
                    if i == DUP_LATE and is_start(b):
                        pe.wait_ge(msg_masked, DUPS)
                    late_products(b, parity, i)
                    if i < NE:
                        early_products(b, parity, i)
                    if e is not None and i == 0:
                        z_transposes(e + BLOCKS, False)

            layer2(0, None, 0)
            with pe.Fori(1, BLOCKS - 1, 2) as b:
                layer2(b, b - 1, 1)
                layer2(b + 1, b, 0)
            z_transposes(last_block + BLOCKS, False)


_INS = ['x', 'adj', 'L0_gnn_item_feat', 'L0_gnn_W_item', 'L0_gnn_b_item', 'L0_gnn_W_user', 'L0_gnn_b_user',
        'L1_gnn_W', 'L1_gnn_B']
_OUTS = [((10000, 128), 'float32')]


def kernel(**inputs):
    import numpy as _np
    import concourse.bacc as _bacc
    from concourse import mybir as _mybir
    from concourse.bass_utils import run_bass_kernel_spmd as _run

    nc = _bacc.Bacc("TRN2", target_bir_lowering=False, num_devices=1)
    arrays, args = {}, []
    for name in _INS:
        a = _np.ascontiguousarray(inputs[name])
        arrays[f"in_{name}_dram"] = a
        args.append(nc.dram_tensor(f"in_{name}_dram", a.shape, _mybir.dt.from_np(a.dtype), kind="ExternalInput").ap())
    for i, (shape, dtype) in enumerate(_OUTS):
        dt = _mybir.dt.from_np(_np.dtype(dtype))
        args.append(nc.dram_tensor(f"out_{i}_dram", shape, dt, kind="ExternalOutput").ap())
    two_graph_layers(nc, *args)
    r = _run(nc, [arrays], core_ids=[0])
    return r.results[0]["out_0_dram"]
```
